# Optimizing a Trainium2 kernel written in Bass

```python
import numpy as np
import jax
import jax.numpy as jnp

def _softmax(x, axis=-1):
    return jax.nn.softmax(x, axis=axis)

def _gelu(x):
    return jax.nn.gelu(x, approximate=True)

def _silu(x):
    return jax.nn.silu(x)

def _sigmoid(x):
    return jax.nn.sigmoid(x)

def _layernorm(x, axis=-1, eps=1e-05):
    m = jnp.mean(x, axis=axis, keepdims=True)
    v = jnp.var(x, axis=axis, keepdims=True)
    return (x - m) / jnp.sqrt(v + eps)

def _scatter_add(tgt, idx, src, axis=0):
    return tgt.at[idx].add(src)

def _segment_sum(src, seg, n):
    return jax.ops.segment_sum(src, seg, n)
kernel_name = 'mk_adaln_ffn_d1_seqx_r4_d3d012'

def setup_inputs(seed: int=0):
    np.random.seed(seed)
    _w = jnp.asarray

    def _rec_inputs():
        import jax
        import jax.numpy as jnp
        _rk = jax.random.key(seed)
        x = -1.394e-06 + 0.9999 * jax.random.normal(jax.random.fold_in(_rk, 1), (4, 512, 512), jnp.float32)
        _lenS = 512 - jax.random.randint(jax.random.fold_in(_rk, 7), (4,), 0, max(1, 512 // 4) + 1, jnp.int32)
        _lenS2 = 512 - jax.random.randint(jax.random.fold_in(_rk, 8), (4,), 0, max(1, 512 // 4) + 1, jnp.int32)
        cond_2048 = -0.00499425 + 1.0058 * jax.random.normal(jax.random.fold_in(_rk, 11), (4, 512), jnp.float32)
        return (x, cond_2048)
    x, cond_2048 = _rec_inputs()

    def _L0_cond_setup():
        import jax, jax.numpy as jnp
        import numpy as np
        B, T, D = (16, 128, 512)
        key = jax.random.key(seed)
        k0, k1, k2, k3 = jax.random.split(key, 4)
        scale = 1.0 / np.sqrt(D)
        return {'initial_state': jax.random.normal(k0, (B, D), jnp.float32), 'inputs': jax.random.normal(k1, (B, T, D), jnp.float32), 'W_ih': jax.random.normal(k2, (D, 3 * D), jnp.float32) * scale, 'W_hh': jax.random.normal(k3, (D, 3 * D), jnp.float32) * scale, 'b_ih': jnp.zeros((3 * D,), jnp.float32), 'b_hh': jnp.zeros((3 * D,), jnp.float32)}
    _L0_cond_all = _L0_cond_setup()
    _L0_cond_in = {k: v for k, v in _L0_cond_all.items() if k in ('W_ih', 'W_hh', 'b_ih', 'b_hh')}
    del _L0_cond_all

    def _L0_ffn_setup():
        import jax, jax.numpy as jnp
        import numpy as np
        B, T, D, E, H = (4, 512, 512, 4, 2048)
        TOPK = 2
        CAPACITY_FACTOR = 1
        key = jax.random.key(seed)
        k0, k1, k2, k3 = jax.random.split(key, 4)
        x = jax.random.normal(k0, (B, T, D), dtype=jnp.float32)
        Wg = jax.random.normal(k1, (D, E), dtype=jnp.float32) * 0.02
        bg = jnp.zeros((E,), dtype=jnp.float32)
        W1 = jax.random.normal(k2, (E, D, H), dtype=jnp.float32) * (1.0 / np.sqrt(D))
        W2 = jax.random.normal(k3, (E, H, D), dtype=jnp.float32) * (1.0 / np.sqrt(H))
        return {'x': x, 'Wg': Wg, 'bg': bg, 'W1': W1, 'W2': W2}
    _L0_ffn_all = _L0_ffn_setup()
    _L0_ffn_in = {k: v for k, v in _L0_ffn_all.items() if k in ('Wg', 'bg', 'W1', 'W2')}
    del _L0_ffn_all
    return {'x': x, 'cond_2048': cond_2048, 'L0_cond_W_ih': _L0_cond_in['W_ih'], 'L0_cond_W_hh': _L0_cond_in['W_hh'], 'L0_cond_b_ih': _L0_cond_in['b_ih'], 'L0_cond_b_hh': _L0_cond_in['b_hh'], 'L0_ffn_Wg': _L0_ffn_in['Wg'], 'L0_ffn_bg': _L0_ffn_in['bg'], 'L0_ffn_W1': _L0_ffn_in['W1'], 'L0_ffn_W2': _L0_ffn_in['W2']}

def reference(x, cond_2048, L0_cond_W_ih, L0_cond_W_hh, L0_cond_b_ih, L0_cond_b_hh, L0_ffn_Wg, L0_ffn_bg, L0_ffn_W1, L0_ffn_W2):
    import jax
    import jax.numpy as jnp

    def _L0_cond_ref(initial_state, inputs, W_ih, W_hh, b_ih, b_hh):
        import jax, jax.numpy as jnp
        import numpy as np
        B, T, D = (16, 128, 512)
        "ScanOverTime(GRU cell): sequential per-timestep module call with\n            dict-state passing; merge_dict_trees stacks the per-step\n            'state_predicted' tensors along axis=1 -> [B, T, D]."

        def cell(h, x):
            gi = x @ W_ih + b_ih
            gh = h @ W_hh + b_hh
            i_r, i_z, i_n = jnp.split(gi, 3, axis=-1)
            h_r, h_z, h_n = jnp.split(gh, 3, axis=-1)
            r = jax.nn.sigmoid(i_r + h_r)
            z = jax.nn.sigmoid(i_z + h_z)
            n = jnp.tanh(i_n + r * h_n)
            h_new = (1.0 - z) * n + z * h
            return (h_new, h_new)
        xs = jnp.swapaxes(inputs, 0, 1)
        _, hs = jax.lax.scan(cell, initial_state, xs)
        return jnp.swapaxes(hs, 0, 1)

    def _L0_ffn_ref(x, Wg, bg, W1, W2):
        import jax, jax.numpy as jnp
        import numpy as np
        B, T, D, E, H = (4, 512, 512, 4, 2048)
        TOPK = 2
        CAPACITY_FACTOR = 1
        Bq, Tq, Dq = x.shape
        N = Bq * Tq
        capacity = int(N * CAPACITY_FACTOR / E)
        flat_x = x.reshape(N, Dq)
        logits = flat_x @ Wg + bg
        top_vals, top_idx = jax.lax.top_k(logits, TOPK)
        sparse = jnp.full_like(logits, -jnp.inf)
        sparse = sparse.at[jnp.arange(N)[:, None], top_idx].set(top_vals)
        probs = jax.nn.softmax(sparse, axis=-1)
        out = jnp.zeros_like(flat_x)
        for i in range(E):
            assigned = (top_idx == i).any(axis=-1)
            score = jnp.where(assigned, probs[:, i], -jnp.inf)
            sel_p, sel_idx = jax.lax.top_k(score, capacity)
            p = jnp.where(jnp.isfinite(sel_p), sel_p, 0.0)[:, None]
            tok = flat_x[sel_idx]
            h = jax.nn.gelu(tok @ W1[i], approximate=False)
            y = h @ W2[i] * p
            out = out.at[sel_idx].add(y)
        return out.reshape(Bq, Tq, Dq)
    x = x + _L0_ffn_ref(_L0_cond_ref(cond_2048, x, L0_cond_W_ih, L0_cond_W_hh, L0_cond_b_ih, L0_cond_b_hh), L0_ffn_Wg, L0_ffn_bg, L0_ffn_W1, L0_ffn_W2)
    return x

_drawn_inputs = setup_inputs


def setup_inputs(seed=0):
    import zlib

    import numpy as np

    out = dict(_drawn_inputs(seed))
    spreads = {'L0_cond_b_ih': (0.0, 0.1), 'L0_cond_b_hh': (0.0, 0.1), 'L0_ffn_bg': (0.0, 0.1)}
    factors = {'cond_2048': 3.948}
    for name, (base, spread) in spreads.items():
        noise = np.random.default_rng([zlib.crc32(name.encode()), seed]).standard_normal(out[name].shape)
        drawn = base * np.exp(spread * noise) if base else spread * noise
        out[name] = jnp.asarray(drawn.astype(out[name].dtype))
    for name, factor in factors.items():
        out[name] = (out[name] * factor).astype(out[name].dtype)
    return out
```

```python
from contextlib import ExitStack

import numpy as np
import concourse.bass as bass
from concourse import mybir

ALU = mybir.AluOpType
ACT = mybir.ActivationFunctionType
AX = mybir.AxisListType
F32 = mybir.dt.float32
F16 = mybir.dt.float16
BF16 = mybir.dt.bfloat16
I32 = mybir.dt.int32

P = 128
SEG = 16
BURN = 20
TOL2 = float(2.0 ** -40)
SEARCH_BITS = 3
SEARCH_PASSES = 10


def gru_moe(nc, x, x_t, cond_t, w_ih, w_hh, b_ih, b_hh, wg, bg, w1, w2, hs_rows, out):
    NB, T, D = x.shape
    N = NB * T
    E, _, H = w1.shape
    CAP = N // E
    L = T // SEG
    COLS = NB * SEG
    KD = D // P
    KH = H // P
    NT = N // P
    NG = CAP // P
    ROW = D + E
    GCOLS = 512
    NC_ = N // GCOLS
    STEPS_C = GCOLS // COLS
    NCAND = 2 ** SEARCH_BITS
    assert COLS == 64 and KD == 4 and BURN % 2 == 0 and BURN <= L and NG == 4 and E == 4

    with ExitStack() as ctx:
        def sb(name, shape, dt=F32):
            return ctx.enter_context(nc.sbuf_tensor(name, shape, dt))

        def sem(name):
            return ctx.enter_context(nc.semaphore(name))

        ps = ctx.enter_context(nc.psum_tensor("ps", [P, 8, 512], F32))

        big = sb("big", [P, 3 * KD * N])
        wa = sb("wa", [P, KD * H])
        wb = sb("wb", [P, KD * 3 * D])
        hx = sb("hx", [P, KD * N])

        gi = big[:, :].rearrange("p (j g c) -> p j g c", j=KD, g=3)
        w2_sb = big[:, 0:KH * D].rearrange("p (k d) -> p k d", k=KH)
        hid = big[:, KH * D:KH * D + KH * CAP].rearrange("p (k c) -> p k c", k=KH)
        rows0 = KH * (D + CAP)
        rows = big[:, rows0:rows0 + 8 * ROW].rearrange("p (n d) -> p n d", n=8)
        y = big[:, rows0:rows0 + NG * D].rearrange("p (g d) -> p g d", g=NG)
        later = [rows0 + 8 * ROW]

        def take(n):
            later[0] += n
            return big[:, later[0] - n:later[0]]
        tokrow = take(NG * ROW).rearrange("p (g d) -> p g d", g=NG)
        cmp4 = take(NT * E * E).rearrange("p (n e f) -> p n e f", n=NT, e=E)
        cmp5 = take(NT * E * E).rearrange("p (n e f) -> p n e f", n=NT, e=E)
        above = take(E * NCAND * NT).rearrange("p (e c n) -> p e c n", e=E, c=NCAND)
        wih_sb = wa[:, 0:KD * 3 * D].rearrange("p (k m) -> p k m", k=KD)
        w1_sb = wa[:, :].rearrange("p (k h) -> p k h", k=KD)
        whh_sb = wb[:, :].rearrange("p (k m) -> p k m", k=KD)
        slots = wb[:, 0:NT * CAP // 2].bitcast(F16).rearrange("p (n c) -> p n c", n=NT)
        tokT = wb[:, NT * CAP // 2:NT * CAP // 2 + KD * CAP].rearrange("p (k c) -> p k c", k=KD)
        xT = hx[:, :].rearrange("p (n k c) -> p n k c", n=NC_, k=KD)
        hsT = hx[:, :].rearrange("p (k c) -> p k c", k=KD)
        hsT_l = hx[:, :].rearrange("p (k c l) -> p k c l", k=KD, l=L)
        assert later[0] <= 3 * KD * N

        ident = sb("ident", [P, P])
        ones = sb("ones", [P, P])
        onesb = sb("onesb", [P, P], BF16)
        before = sb("before", [P, P], BF16)
        bih = sb("bih", [P, 12])
        bhh = sb("bhh", [P, 12])
        bsum = sb("bsum", [P, 12])
        h0 = sb("h0", [P, KD, NB])
        wg_sb = sb("wg_sb", [P, KD, E])
        bg_sb = sb("bg_sb", [P, E])
        state = sb("state", [P, 2, KD * COLS])
        start = sb("start", [P, KD * COLS])
        pre = sb("pre", [P, KD, 2, COLS])
        rz = sb("rz", [P, KD, 2, COLS])
        rn = sb("rn", [P, KD, COLS])
        cand_in = sb("cand_in", [P, KD, COLS])
        cand = sb("cand", [P, KD, COLS])
        zh = sb("zh", [P, KD, COLS])
        ocand = sb("ocand", [P, KD, COLS])
        dsq = sb("dsq", [P, KD * NB, SEG])
        hsq = sb("hsq", [P, KD * COLS])
        worst = sb("worst", [P, 4])
        flag = sb("flag", [P, SEG + 2], I32)
        lg = sb("lg", [P, NT, E])
        earlier = sb("earlier", [P, E, E])
        rank = sb("rank", [P, NT, E])
        lmax = sb("lmax", [P, NT])
        wsum = sb("wsum", [P, NT])
        prob = sb("prob", [P, NT, E])
        score = sb("score", [P, E, NT])
        steps_i = sb("steps_i", [P, SEARCH_PASSES, NCAND], I32)
        trial = sb("trial", [P, E, NCAND], I32)
        nabove = sb("nabove", [P, E, NCAND])
        keep = sb("keep", [P, E, NCAND])
        thr = sb("thr", [P, E])
        gt = sb("gt", [P, E, NT], BF16)
        eqp = sb("eqp", [P, E, 2 * NT], BF16)
        selp = sb("selp", [P, E, 2 * NT], BF16)
        fits = sb("fits", [P, E, NT], BF16)
        pos = sb("pos", [P, E, NT])
        slot_no = sb("slot_no", [P, CAP], F16)
        tok_id = sb("tok_id", [P, NT], F16)
        idx = sb("idx", [P, NG], I32)
        idx_out = sb("idx_out", [P, NG], I32)
        p_out = sb("p_out", [P, NG])

        state3 = [state[:, i, :].rearrange("p (k c) -> p k c", k=KD) for i in range(2)]
        state_s = state[:, 0, :].rearrange("p (kb s) -> p kb s", s=SEG)
        start_s = start[:, :].rearrange("p (kb s) -> p kb s", s=SEG)
        gate_ps = ps[:, 0:4, 0:3 * COLS].rearrange("p j (g c) -> p j g c", g=3)

        names = """small_loaded whh_loaded x_loaded out_init consts_pool consts_dve bias_ready
             gi_mm gi_ready h_ready gates_mm pre_ready sig_done rn_done
            candin_ready tanh_done ocand_done copied start_saved check_a worst_ready worst_mm flag_written flag_ready
            gru_over logits_mm route turned rows_ready rows_copied rows_stored exp_in exp_done
            prob_ready nabove_ready total_mm masks_ready eq_mm sel_ready pos_mm pos_ready slots_ready list_mm idx_ready
            gathered tok_turned tokT_ready ffn1_mm hid_ready ffn2_mm y_ready scattered latched w1_loaded w2_loaded
            tables sp_waited pool_waited dve_waited pe_waited act_waited pool_consts""".split()
        S = {name: sem(name) for name in names}
        S["wih_loaded"] = [sem(f"wih_loaded_{g}") for g in range(3)]
        block = ctx.enter_context(nc.Block())

        whh_src = w_hh.rearrange("(k p) m -> p k m", p=P)
        wih_src = w_ih.rearrange("(k p) m -> p k m", p=P)
        w1_src = w1.rearrange("e (k p) h -> e p k h", p=P)
        w2_src = w2.rearrange("e (k p) d -> e p k d", p=P)
        rows_dst = hs_rows.rearrange("(n p) d -> n p d", p=P)

        @block.sync
        def _(sp):
            sp.dma_start(xT[:, 0, :, :], x_t[:, 0, :, :]).then_inc(S["x_loaded"], 16)
            for g in range(3):
                sp.dma_start(wih_sb[:, :, g * D:(g + 1) * D], wih_src[:, :, g * D:(g + 1) * D]
                             ).then_inc(S["wih_loaded"][g], 16)
            for n in range(1, NC_):
                sp.wait_ge(S["x_loaded"], 16 * n)
                sp.dma_start(xT[:, n, :, :], x_t[:, n, :, :]).then_inc(S["x_loaded"], 16)
            for k in range(KD):
                sp.dma_start(whh_sb[:, k, :], whh_src[:, k, :]).then_inc(S["whh_loaded"], 16)
            sp.dma_start(out.rearrange("b t d -> (b t) d"), x.rearrange("b t d -> (b t) d")).then_inc(S["out_init"], 16)
            sp.wait_ge(S["gi_mm"], 12 * NC_)
            for k in range(KD):
                sp.dma_start(w1_sb[:, k, :], w1_src[0, :, k, :]).then_inc(S["w1_loaded"], 16)
            sp.wait_ge(S["gru_over"], 1)
            for k in range(4):
                sp.dma_start(w2_sb[:, 4 * k:4 * k + 4, :], w2_src[0, :, 4 * k:4 * k + 4, :]).then_inc(S["w2_loaded"], 16)
            for n in range(NT):
                sp.wait_ge(S["rows_ready"], n + 1)
                if n == 0:
                    sp.wait_ge(S["prob_ready"], 1)
                sp.dma_start(rows_dst[n], rows[:, n % 8, :]).then_inc(S["rows_stored"], 16)
            with sp.Fori(1, E) as e:
                sp.wait_ge(S["ffn1_mm"], KH * e)
                sp.sem_inc(S["sp_waited"], 1)
                for k in range(KD):
                    sp.dma_start(w1_sb[:, k, :],
                                 w1_src[bass.ds(e, 1), :, k, :].rearrange("o p h -> (o p) h")).then_inc(S["w1_loaded"], 16)
                sp.wait_ge(S["ffn2_mm"], NG * e)
                sp.sem_inc(S["sp_waited"], 1)
                for k in range(4):
                    sp.dma_start(w2_sb[:, 4 * k:4 * k + 4, :],
                                 w2_src[bass.ds(e, 1), :, 4 * k:4 * k + 4, :].rearrange("o p k d -> (o p) k d")
                                 ).then_inc(S["w2_loaded"], 16)
            sp.wait_ge(S["out_init"], 16)
            sp.wait_ge(S["rows_stored"], 16 * NT)
            sp.wait_ge(S["scattered"], 16 * NG * E)

        @block.tensor
        def _(pe):
            pe.wait_ge(S["consts_pool"], 1)
            with pe.Fori(0, NC_) as c:
                pe.wait_ge(S["x_loaded"], c * 16 + 16)
                for m in range(12):
                    if m >= 2:
                        pe.wait_ge(S["gi_ready"], c * 12 + m - 1)
                    if m % 4 == 0:
                        pe.wait_ge(S["wih_loaded"][m // 4], 16)
                    for k in range(KD):
                        mm = pe.matmul(ps[:, 2 + m % 2, :], wih_sb[:, k, m * P:(m + 1) * P],
                                       xT[:, bass.ds(c, 1), k, :].rearrange("p o c -> p (o c)"), start=(k == 0), stop=(k == KD - 1))
                    mm.then_inc(S["gi_mm"], 1)
                pe.wait_ge(S["gi_ready"], c * 12 + 12)

            def gates(src, base):
                have = [0]

                def part(j, ks):
                    for k in ks:
                        if k >= have[0]:
                            pe.wait_ge(S["h_ready"], base + k + 1)
                            have[0] = k + 1
                        for g in range(3):
                            mm = pe.matmul(gate_ps[:, j, g, :], whh_sb[:, k, (4 * g + j) * P:(4 * g + j + 1) * P],
                                           state3[src][:, k, :], start=(k == 0 and g == 0), stop=(k == KD - 1),
                                           skip_group_check=True)
                    if ks[-1] == KD - 1:
                        mm.then_inc(S["gates_mm"], 1)
                part(0, [0, 1])
                part(1, [0, 1])
                part(0, [2])
                part(1, [2])
                part(0, [3])
                part(1, [3])
                part(2, [0, 1, 2, 3])
                part(3, [0, 1, 2, 3])

            pe.wait_ge(S["whh_loaded"], 16 * KD)
            with pe.Fori(0, BURN // 2) as i:
                for u in range(2):
                    gates(u, 8 * i + 4 * u)
            with pe.Fori(0, SEG) as r:
                pe.wait_ge(S["flag_ready"], r + 1)
                pe.sem_inc(S["pe_waited"], 1)
                go = pe.value_load(flag[0:1, bass.ds(r, 1)])
                with pe.If(go > 0):
                    with pe.Fori(0, L // 2) as i:
                        for u in range(2):
                            gates(u, r * (4 * L + 4) + 8 * i + (4 * BURN + 4 + 4 * u))
                    pe.wait_ge(S["worst_ready"], r + 1)
                    pe.matmul(ps[0:1, 4, 0:1], worst[:, 2:3], ones[:, 0:1], start=True, stop=True).then_inc(S["worst_mm"], 1)

            pe.wait_ge(S["gru_over"], 1)
            pe.wait_ge(S["small_loaded"], 16 * 5)
            for n in range(NT):
                for k in range(KD):
                    mm = pe.matmul(ps[:, 5, n * E:(n + 1) * E], hsT[:, k, n * P:(n + 1) * P], wg_sb[:, k, :],
                                   start=(k == 0), stop=(k == KD - 1))
            mm.then_inc(S["logits_mm"], 1)
            for n in range(NT):
                if n >= 2:
                    pe.wait_ge(S["rows_copied"], n - 1)
                for k in range(KD):
                    mm = pe.transpose(ps[:, n % 2, k * P:(k + 1) * P], hsT[:, k, n * P:(n + 1) * P], ident[:, :])
                mm.then_inc(S["turned"], 1)
            with pe.Fori(0, SEARCH_PASSES) as i:
                pe.wait_ge(S["nabove_ready"], i + 1)
                pe.matmul(ps[:, 6, 0:E * NCAND], ones[:, :], nabove[:, :, :].rearrange("p e c -> p (e c)"),
                          start=True, stop=True).then_inc(S["total_mm"], 1)

            def earlier_count(bank, maskp, more):
                o = ps[:, bank, 0:E * NT].rearrange("p (e n) -> p e n", e=E)
                pe.matmul(o, before[:, :], maskp[:, :, NT:2 * NT], start=True, stop=False)
                for d in range(1, NT):
                    mm = pe.matmul(o, onesb[:, :], maskp[:, :, NT - d:2 * NT - d], start=False,
                                   stop=(d == NT - 1 and not more))
                if more:
                    for n in range(NT):
                        mm = pe.matmul(o, onesb[:, :], gt[:, :, n:n + 1].to_broadcast([P, E, NT]), start=False,
                                       stop=(n == NT - 1))
                return mm

            pe.wait_ge(S["masks_ready"], 1)
            earlier_count(7, eqp, True).then_inc(S["eq_mm"], 1)
            pe.wait_ge(S["sel_ready"], 1)
            earlier_count(7, selp, False).then_inc(S["pos_mm"], 1)

            def token_list(e):
                pe.wait_ge(S["slots_ready"], NT * e + NT)
                for n in range(NT):
                    for g in range(NG):
                        mm = pe.matmul(ps[:, 6, g:g + 1], slots[:, n, g * P:(g + 1) * P], tok_id[:, n:n + 1],
                                       start=(n == 0 and g == 0), stop=(n == NT - 1), skip_group_check=True)
                mm.then_inc(S["list_mm"], 1)

            def turn_tokens(e):
                pe.wait_ge(S["gathered"], 16 * NG * e + 16 * NG)
                for g in range(NG):
                    if g >= 2:
                        pe.wait_ge(S["tokT_ready"], NG * e + g - 1)
                    for k in range(KD):
                        mm = pe.transpose(ps[:, 4 + g % 2, k * P:(k + 1) * P], tokrow[:, g, k * P:(k + 1) * P],
                                          ident[:, :])
                    mm.then_inc(S["tok_turned"], 1)

            def expert(e, last):
                pe.wait_ge(S["tokT_ready"], NG * e + NG)
                pe.wait_ge(S["w1_loaded"], 16 * KD * e + 16 * KD)
                for m in range(KH):
                    if m >= 2:
                        pe.wait_ge(S["hid_ready"], KH * e + m - 1)
                    for k in range(KD):
                        mm = pe.matmul(ps[:, m % 2, :], w1_sb[:, k, m * P:(m + 1) * P], tokT[:, k, :],
                                       start=(k == 0), stop=(k == KD - 1))
                    mm.then_inc(S["ffn1_mm"], 1)
                if not last:
                    token_list(e + 1)
                pe.wait_ge(S["hid_ready"], KH * e + KH)
                pe.wait_ge(S["w2_loaded"], 64 * e + 64)
                for g in range(NG):
                    if g >= 2:
                        pe.wait_ge(S["y_ready"], NG * e + g - 1)
                    for k in range(KH):
                        mm = pe.matmul(ps[:, 2 + g % 2, :], hid[:, k, g * P:(g + 1) * P], w2_sb[:, k, :],
                                       start=(k == 0), stop=(k == KH - 1))
                    mm.then_inc(S["ffn2_mm"], 1)
                    if g == 1 and not last:
                        turn_tokens(e + 1)
                pe.wait_ge(S["y_ready"], NG * e + NG)

            token_list(0)
            turn_tokens(0)
            with pe.Fori(0, E - 1) as e:
                expert(e, False)
            expert(E - 1, True)

        @block.scalar
        def _(act):
            act.dma_start(bih[:, :], b_ih).then_inc(S["small_loaded"], 16)
            act.dma_start(bhh[:, :], b_hh).then_inc(S["small_loaded"], 16)
            act.dma_start(h0[:, :, :], cond_t).then_inc(S["small_loaded"], 16)
            act.dma_start(wg_sb[:, :, :], wg).then_inc(S["small_loaded"], 16)
            act.dma_start(bg_sb[:, :], bg.rearrange("(o e) -> o e", o=1).to_broadcast([P, E])).then_inc(S["small_loaded"], 16)
            act.wait_ge(S["consts_dve"], 1)
            act.activation(cand[:, 0, 0:1], ones[:, 0:1], ACT.Sigmoid).then_inc(S["tables"], 1)
            act.wait_ge(S["tables"], 1)

            def step(base):
                def sig(j):
                    act.wait_ge(S["pre_ready"], base + j + 1)
                    act.activation(rz[:, j, :, :], pre[:, j, :, :], ACT.Sigmoid).then_inc(S["sig_done"], 1)

                def tanh(j):
                    act.wait_ge(S["candin_ready"], base + j + 1)
                    act.activation(cand[:, j, :], cand_in[:, j, :], ACT.Tanh).then_inc(S["tanh_done"], 1)
                for f, j in ((sig, 0), (sig, 1), (tanh, 0), (tanh, 1), (sig, 2), (tanh, 2), (sig, 3), (tanh, 3)):
                    f(j)

            with act.Fori(0, BURN // 2) as i:
                for u in range(2):
                    step(8 * i + 4 * u)
            with act.Fori(0, SEG) as r:
                act.wait_ge(S["flag_ready"], r + 1)
                act.sem_inc(S["act_waited"], 1)
                go = act.value_load(flag[0:1, bass.ds(r, 1)])
                with act.If(go > 0):
                    with act.Fori(0, L // 2) as i:
                        for u in range(2):
                            step(4 * L * r + 8 * i + (4 * BURN + 4 * u))

            for n in range(NT):
                act.wait_ge(S["turned"], n + 1)
                if n == 0:
                    act.wait_ge(S["gru_over"], 1)
                if n >= 8:
                    act.wait_ge(S["rows_stored"], 16 * NT // 2)
                act.copy(rows[:, n % 8, 0:D], ps[:, n % 2, :]).then_inc(S["rows_copied"], 1)
                if n == 3:
                    act.wait_ge(S["exp_in"], 1)
                    act.activation(prob[:, :, :], lg[:, :, :], ACT.Exp).then_inc(S["exp_done"], 1)

            def gelu(e):
                for m in range(KH):
                    act.wait_ge(S["ffn1_mm"], KH * e + m + 1)
                    act.activation(hid[:, m, :], ps[:, m % 2, :], ACT.Gelu).then_inc(S["hid_ready"], 1)
            with act.Fori(0, E) as e:
                gelu(e)

        @block.gpsimd
        def _(pool):
            pool.memset(ident[:, :], 0.0).then_inc(S["pool_consts"], 1)
            pool.wait_ge(S["pool_consts"], 1)
            pool.affine_select(out=ident[:, :], in_=ident[:, :], compare_op=ALU.not_equal, fill=1.0, base=0,
                               pattern=[[-1, P]], channel_multiplier=1).then_inc(S["consts_pool"], 1)
            pool.memset(before[:, :], 0.0).then_inc(S["pool_consts"], 1)
            pool.wait_ge(S["pool_consts"], 2)
            pool.affine_select(out=before[:, :], in_=before[:, :], compare_op=ALU.is_ge, fill=1.0, base=0,
                               pattern=[[-1, P]], channel_multiplier=1).then_inc(S["consts_pool"], 1)
            pool.iota(slot_no[:, :], [[1, CAP]], base=0, channel_multiplier=0,
                      allow_small_or_imprecise_dtypes=True).then_inc(S["consts_pool"], 1)
            pool.iota(tok_id[:, :], [[P, NT]], base=0, channel_multiplier=1,
                      allow_small_or_imprecise_dtypes=True).then_inc(S["consts_pool"], 1)
            pool.memset(earlier[:, :, :], 0.0).then_inc(S["pool_consts"], 1)
            pool.wait_ge(S["pool_consts"], 3)
            pool.affine_select(out=earlier[:, :, :], in_=earlier[:, :, :], compare_op=ALU.is_ge, fill=1.0, base=0,
                               pattern=[[-1, E], [1, E]], channel_multiplier=0).then_inc(S["consts_pool"], 1)
            pool.memset(worst[:, 3:4], 0.0).then_inc(S["copied"], 2)

            with pool.Fori(0, SEG) as r:
                pool.wait_ge(S["flag_ready"], r + 1)
                pool.sem_inc(S["pool_waited"], 1)
                go = pool.value_load(flag[0:1, bass.ds(r, 1)])
                with pool.If(go > 0):
                    with pool.Fori(0, L // 2) as i:
                        for u in range(2):
                            pool.wait_ge(S["h_ready"], r * (4 * L + 4) + 8 * i + (4 * BURN + 12 + 4 * u))
                            pool.tensor_copy(
                                hsT_l[:, :, :, bass.ds(2 * i + u, 1)].rearrange("p k c o -> p k (c o)"),
                                state3[1 - u]).then_inc(S["copied"], 1)

            def gather(e):
                pool.wait_ge(S["idx_ready"], e + 1)
                pool.sem_inc(S["pool_waited"], 1)
                for g in range(NG):
                    pool.indirect_dma_start(
                        out=tokrow[:, g, :], out_offset=None, in_=hs_rows,
                        in_offset=bass.IndirectOffsetOnAxis(ap=idx[:, g:g + 1], axis=0)).then_inc(S["gathered"], 16)

            def scatter(e):
                for g in range(NG):
                    pool.wait_ge(S["y_ready"], NG * e + g + 1)
                    pool.sem_inc(S["pool_waited"], 1)
                    pool.indirect_dma_start(
                        out=out.rearrange("b t d -> (b t) d"),
                        out_offset=bass.IndirectOffsetOnAxis(ap=idx_out[:, g:g + 1], axis=0),
                        in_=y[:, g, :], in_offset=None, compute_op=ALU.add).then_inc(S["scattered"], 16)

            pool.wait_ge(S["rows_stored"], 16 * NT)
            pool.wait_ge(S["out_init"], 16)
            gather(0)
            with pool.Fori(0, E - 1) as e:
                pool.wait_ge(S["latched"], e + 1)
                pool.sem_inc(S["pool_waited"], 1)
                gather(e + 1)
                scatter(e)
            scatter(E - 1)

        @block.vector
        def _(dve):
            dve.memset(ones[:, :], 1.0).then_inc(S["consts_dve"], 1)
            dve.memset(onesb[:, :], 1.0)
            dve.memset(flag[:, :], 0)
            dve.memset(eqp[:, :, 0:NT], 0.0)
            dve.memset(selp[:, :, 0:NT], 0.0)
            dve.memset(state[:, 0, :], 0.0).then_inc(S["h_ready"], 4)
            dve.wait_ge(S["small_loaded"], 16 * 5)
            dve.tensor_tensor(bsum[:, 0:8], bih[:, 0:8], bhh[:, 0:8], ALU.add)
            dve.tensor_copy(bsum[:, 8:12], bih[:, 8:12]).then_inc(S["bias_ready"], 1)
            dve.wait_ge(S["bias_ready"], 1)

            with dve.Fori(0, NC_) as c:
                for m in range(12):
                    dve.wait_ge(S["gi_mm"], c * 12 + m + 1)
                    dve.tensor_scalar(gi[:, m % 4, m // 4, bass.ds(c * GCOLS, GCOLS)], ps[:, 2 + m % 2, :],
                                      bsum[:, m:m + 1], None, ALU.add).then_inc(S["gi_ready"], 1)
            dve.wait_ge(S["gi_ready"], 12 * NC_)

            def step(src, l, base, wait_copy):
                col = l * COLS

                def pre_rz(j):
                    dve.wait_ge(S["gates_mm"], base + j + 1)
                    dve.tensor_tensor(pre[:, j, :, :], gate_ps[:, j, 0:2, :], gi[:, j, 0:2, bass.ds(col, COLS)],
                                      ALU.add).then_inc(S["pre_ready"], 1)

                def candidate_in(j):
                    dve.wait_ge(S["sig_done"], base + j + 1)
                    dve.scalar_tensor_tensor(rn[:, j, :], gate_ps[:, j, 2, :], bhh[:, 8 + j:9 + j], rz[:, j, 0, :],
                                             ALU.add, ALU.mult).then_inc(S["rn_done"], 1)
                    dve.tensor_tensor(zh[:, j, :], rz[:, j, 1, :], state3[src][:, j, :], ALU.mult)
                    dve.wait_ge(S["rn_done"], base + j + 1)
                    dve.tensor_tensor(cand_in[:, j, :], rn[:, j, :], gi[:, j, 2, bass.ds(col, COLS)],
                                      ALU.add).then_inc(S["candin_ready"], 1)

                def blend(j):
                    dve.wait_ge(S["tanh_done"], base + j + 1)
                    dve.scalar_tensor_tensor(ocand[:, j, :], rz[:, j, 1, :], -1.0, cand[:, j, :],
                                             ALU.add, ALU.mult).then_inc(S["ocand_done"], 1)
                    if j == 0 and wait_copy is not None:
                        dve.wait_ge(S["copied"], wait_copy)
                    dve.wait_ge(S["ocand_done"], base + j + 1)
                    dve.tensor_tensor(state3[1 - src][:, j, :], zh[:, j, :], ocand[:, j, :],
                                      ALU.subtract).then_inc(S["h_ready"], 1)
                pre_rz(0)
                pre_rz(1)
                candidate_in(0)
                candidate_in(1)
                blend(0)
                blend(1)
                pre_rz(2)
                candidate_in(2)
                pre_rz(3)
                blend(2)
                candidate_in(3)
                blend(3)

            def next_start(count):
                dve.tensor_copy(start_s[:, :, 1:SEG], state_s[:, :, 0:SEG - 1]).then_inc(S["start_saved"], 1)
                dve.wait_ge(S["start_saved"], count)
                dve.tensor_copy(state[:, 0, :], start[:, :]).then_inc(S["h_ready"], 4)

            with dve.Fori(0, BURN // 2) as i:
                for u in range(2):
                    step(u, 2 * i + (L - BURN + u), 8 * i + 4 * u, None)
            dve.wait_ge(S["h_ready"], 4 * BURN + 4)
            dve.tensor_copy(start_s[:, :, 0:1], h0[:, :, :].rearrange("p k b -> p (k b)").unsqueeze(2))
            next_start(1)
            dve.memset(flag[:, 0:1], 1).then_inc(S["flag_written"], 1)
            dve.wait_ge(S["flag_written"], 1)
            dve.sem_inc(S["flag_ready"], 1)

            with dve.Fori(0, SEG) as r:
                dve.wait_ge(S["flag_ready"], r + 1)
                dve.sem_inc(S["dve_waited"], 1)
                go = dve.value_load(flag[0:1, bass.ds(r, 1)])
                with dve.If(go > 0):
                    with dve.Fori(0, L // 2) as i:
                        for u in range(2):
                            step(u, 2 * i + u, 4 * L * r + 8 * i + (4 * BURN + 4 * u), L * r + 2 * i + (u + 1))
                    dve.wait_ge(S["h_ready"], r * (4 * L + 4) + (4 * BURN + 8 + 4 * L))
                    dve.tensor_tensor(dsq[:, :, 0:SEG - 1], state_s[:, :, 0:SEG - 1], start_s[:, :, 1:SEG],
                                      ALU.subtract).then_inc(S["check_a"], 1)
                    dve.tensor_tensor(hsq[:, :], state[:, 0, :], state[:, 0, :], ALU.mult).then_inc(S["check_a"], 1)
                    dve.wait_ge(S["check_a"], 6 * r + 2)
                    dve.tensor_tensor(dsq[:, :, 0:SEG - 1], dsq[:, :, 0:SEG - 1], dsq[:, :, 0:SEG - 1],
                                      ALU.mult).then_inc(S["check_a"], 1)
                    dve.tensor_reduce(worst[:, 1:2], hsq[:, :], AX.X, ALU.max).then_inc(S["check_a"], 1)
                    dve.wait_ge(S["check_a"], 6 * r + 4)
                    dve.tensor_reduce(worst[:, 0:1], dsq[:, :, 0:SEG - 1], AX.XY, ALU.max).then_inc(S["check_a"], 1)
                    dve.wait_ge(S["check_a"], 6 * r + 5)
                    dve.scalar_tensor_tensor(worst[:, 2:3], worst[:, 1:2], TOL2, worst[:, 0:1],
                                             ALU.mult, ALU.is_lt).then_inc(S["worst_ready"], 1)
                    dve.wait_ge(S["copied"], L * r + (L + 2))
                    next_start(r + 2)
                    dve.wait_ge(S["worst_mm"], r + 1)
                    dve.tensor_copy(flag[0:1, bass.ds(r + 1, 1)], ps[0:1, 4, 0:1]).then_inc(S["check_a"], 1)
                    dve.wait_ge(S["check_a"], 6 * r + 6)
                    dve.sem_inc(S["flag_written"], 1)
                dve.sem_inc(S["flag_ready"], 1)
            dve.sem_inc(S["gru_over"], 1)

            dve.wait_ge(S["consts_pool"], 5)
            dve.wait_ge(S["logits_mm"], 1)
            done = [0]

            def link(ins):
                done[0] += 1
                ins.then_inc(S["route"], 1)
                dve.wait_ge(S["route"], done[0])
            lgp = ps[:, 5, 0:NT * E].rearrange("p (n e) -> p n e", n=NT)
            mine = lg[:, :, :].unsqueeze(3).to_broadcast([P, NT, E, E])
            other = lg[:, :, :].unsqueeze(2).to_broadcast([P, NT, E, E])
            link(dve.tensor_tensor(lg[:, :, :], lgp, bg_sb[:, :].unsqueeze(1).to_broadcast([P, NT, E]), ALU.add))
            dve.tensor_tensor(cmp4[:, :, :, :], other, mine, ALU.is_gt)
            dve.tensor_tensor(cmp5[:, :, :, :], other, mine, ALU.is_equal)
            link(dve.tensor_reduce(lmax[:, :], lg[:, :, :], AX.X, ALU.max))
            link(dve.tensor_tensor(cmp5[:, :, :, :], cmp5[:, :, :, :],
                                   earlier[:, :, :].unsqueeze(1).to_broadcast([P, NT, E, E]), ALU.mult))
            dve.tensor_tensor(lg[:, :, :], lg[:, :, :], lmax[:, :].unsqueeze(2).to_broadcast([P, NT, E]),
                              ALU.subtract).then_inc(S["exp_in"], 1)
            link(dve.tensor_tensor(cmp4[:, :, :, :], cmp4[:, :, :, :], cmp5[:, :, :, :], ALU.add))
            link(dve.tensor_reduce(rank[:, :, :], cmp4[:, :, :, :], AX.X, ALU.add))
            dve.wait_ge(S["exp_done"], 1)
            link(dve.scalar_tensor_tensor(prob[:, :, :], rank[:, :, :], 2.0, prob[:, :, :], ALU.is_lt, ALU.mult))
            link(dve.tensor_reduce(wsum[:, :], prob[:, :, :], AX.X, ALU.add))
            link(dve.reciprocal(wsum[:, :], wsum[:, :]))
            link(dve.tensor_tensor(prob[:, :, :], prob[:, :, :], wsum[:, :].unsqueeze(2).to_broadcast([P, NT, E]),
                                   ALU.mult))
            dve.tensor_copy(score[:, :, :], prob[:, :, :].rearrange("p n e -> p e n"))
            link(dve.memset(thr[:, :], 0.0))
            for n in range(NT):
                dve.wait_ge(S["rows_copied"], n + 1)
                ins = dve.tensor_copy(rows[:, n % 8, D:ROW], prob[:, n, :])
                ins.then_inc(S["rows_ready"], 1)
                if n == 0:
                    dve.sem_inc(S["prob_ready"], 1)

            for i in range(SEARCH_PASSES):
                shift = SEARCH_BITS * (SEARCH_PASSES - 1 - i)
                for c in range(NCAND):
                    ins = dve.memset(steps_i[:, i, c:c + 1], c << shift)
            link(ins)
            with dve.Fori(0, SEARCH_PASSES) as i:
                base = done[0]
                dve.tensor_tensor(trial[:, :, :], thr[:, :].bitcast(I32).unsqueeze(2).to_broadcast([P, E, NCAND]),
                                  steps_i[:, bass.ds(i, 1), :].to_broadcast([P, E, NCAND]),
                                  ALU.bitwise_or).then_inc(S["route"], 1)
                dve.wait_ge(S["route"], 4 * i + (base + 1))
                dve.tensor_tensor(above[:, :, :, :], score[:, :, :].unsqueeze(2).to_broadcast([P, E, NCAND, NT]),
                                  trial[:, :, :].bitcast(F32).unsqueeze(3).to_broadcast([P, E, NCAND, NT]),
                                  ALU.is_ge).then_inc(S["route"], 1)
                dve.wait_ge(S["route"], 4 * i + (base + 2))
                dve.tensor_reduce(nabove[:, :, :], above[:, :, :, :], AX.X, ALU.add).then_inc(S["nabove_ready"], 1)
                dve.wait_ge(S["total_mm"], i + 1)
                dve.scalar_tensor_tensor(keep[:, :, :], ps[:, 6, 0:E * NCAND].rearrange("p (e c) -> p e c", e=E),
                                         float(CAP), trial[:, :, :].bitcast(F32), ALU.is_ge,
                                         ALU.mult).then_inc(S["route"], 1)
                dve.wait_ge(S["route"], 4 * i + (base + 3))
                dve.tensor_reduce(thr[:, :], keep[:, :, :], AX.X, ALU.max).then_inc(S["route"], 1)
                dve.wait_ge(S["route"], 4 * i + (base + 4))
            done[0] += 4 * SEARCH_PASSES

            thr_b = thr[:, :].unsqueeze(2).to_broadcast([P, E, NT])
            ps7 = ps[:, 7, 0:E * NT].rearrange("p (e n) -> p e n", e=E)
            dve.tensor_tensor(gt[:, :, :], score[:, :, :], thr_b, ALU.is_gt)
            link(dve.tensor_tensor(eqp[:, :, NT:2 * NT], score[:, :, :], thr_b, ALU.is_equal))
            dve.sem_inc(S["masks_ready"], 1)
            dve.wait_ge(S["eq_mm"], 1)
            link(dve.scalar_tensor_tensor(fits[:, :, :], ps7, float(CAP), eqp[:, :, NT:2 * NT], ALU.is_lt, ALU.mult))
            link(dve.tensor_tensor(selp[:, :, NT:2 * NT], fits[:, :, :], gt[:, :, :], ALU.add))
            dve.sem_inc(S["sel_ready"], 1)
            dve.wait_ge(S["pos_mm"], 1)
            link(dve.scalar_tensor_tensor(pos[:, :, :], ps7, 1.0, selp[:, :, NT:2 * NT], ALU.add, ALU.mult))
            link(dve.tensor_scalar(pos[:, :, :], pos[:, :, :], -1.0, None, ALU.add))

            def one_hot(e):
                for n in range(NT):
                    dve.tensor_scalar(slots[:, n, :], slot_no[:, :], pos[:, bass.ds(e, 1), n:n + 1].rearrange("p o n -> p (o n)"),
                                      None, ALU.is_equal).then_inc(S["slots_ready"], 1)

            def make_idx(e):
                dve.wait_ge(S["list_mm"], e + 1)
                dve.tensor_copy(idx[:, :], ps[:, 6, 0:NG]).then_inc(S["idx_ready"], 1)

            def tokens_T(e):
                for g in range(NG):
                    dve.wait_ge(S["tok_turned"], NG * e + g + 1)
                    dve.tensor_copy(tokT[:, :, g * P:(g + 1) * P],
                                    ps[:, 4 + g % 2, :].rearrange("p (k c) -> p k c", k=KD)).then_inc(S["tokT_ready"], 1)

            def latch(e):
                dve.tensor_copy(idx_out[:, :], idx[:, :])
                dve.tensor_copy(p_out[:, :], tokrow[:, :, bass.ds(D + e, 1)].rearrange("p g o -> p (g o)")
                                ).then_inc(S["latched"], 1)
                dve.wait_ge(S["latched"], e + 1)

            def weigh(e, g):
                dve.wait_ge(S["ffn2_mm"], NG * e + g + 1)
                dve.tensor_scalar(y[:, g, :], ps[:, 2 + g % 2, :], p_out[:, g:g + 1], None,
                                  ALU.mult).then_inc(S["y_ready"], 1)

            one_hot(0)
            make_idx(0)
            tokens_T(0)
            latch(0)
            with dve.Fori(0, E - 1) as e:
                one_hot(e + 1)
                make_idx(e + 1)
                weigh(e, 0)
                weigh(e, 1)
                tokens_T(e + 1)
                weigh(e, 2)
                weigh(e, 3)
                dve.wait_ge(S["scattered"], 16 * NG * e + 16 * NG)
                latch(e + 1)
            for g in range(NG):
                weigh(E - 1, g)


def laid_out(inputs):
    x = np.asarray(inputs['x'])
    nb, t, d = x.shape
    kd, steps = d // P, t // SEG
    x_t = x.reshape(nb * SEG, steps, kd, P).transpose(3, 2, 1, 0).reshape(P, kd, -1, 512).transpose(0, 2, 1, 3)
    return {
        'x': x,
        'x_t': x_t,
        'cond_t': np.asarray(inputs['cond_2048']).reshape(nb, kd, P).transpose(2, 1, 0),
        'w_ih': inputs['L0_cond_W_ih'],
        'w_hh': inputs['L0_cond_W_hh'],
        'b_ih': np.asarray(inputs['L0_cond_b_ih']).reshape(-1, P).T,
        'b_hh': np.asarray(inputs['L0_cond_b_hh']).reshape(-1, P).T,
        'wg': np.asarray(inputs['L0_ffn_Wg']).reshape(kd, P, -1).transpose(1, 0, 2),
        'bg': inputs['L0_ffn_bg'],
        'w1': inputs['L0_ffn_W1'],
        'w2': inputs['L0_ffn_W2'],
    }


def kernel(**inputs):
    import concourse.bacc as bacc
    from concourse.bass_utils import run_bass_kernel_spmd

    nc = bacc.Bacc("TRN2", target_bir_lowering=False, num_devices=1)
    arrays, args = {}, []
    for name, a in laid_out(inputs).items():
        a = np.ascontiguousarray(a)
        arrays[f"in_{name}"] = a
        args.append(nc.dram_tensor(f"in_{name}", a.shape, mybir.dt.from_np(a.dtype), kind="ExternalInput").ap())
    shape = inputs['x'].shape
    experts = inputs['L0_ffn_Wg'].shape[1]
    hs_rows = nc.dram_tensor("hs_rows", (shape[0] * shape[1], shape[2] + experts), F32, kind="Internal").ap()
    out = nc.dram_tensor("out_0", shape, F32, kind="ExternalOutput").ap()
    gru_moe(nc, *args, hs_rows, out)
    r = run_bass_kernel_spmd(nc, [arrays], core_ids=[0])
    return r.results[0]["out_0"]
```

```python
from contextlib import ExitStack

import numpy as np
import concourse.bass as bass
from concourse import mybir

ALU = mybir.AluOpType
ACT = mybir.ActivationFunctionType
AX = mybir.AxisListType
RMAX = bass.bass_isa.ReduceOp.max
F32 = mybir.dt.float32
F16 = mybir.dt.float16
BF16 = mybir.dt.bfloat16
I32 = mybir.dt.int32

P = 128
SEG = 16
BURN = 20
TOL2 = float(2.0 ** -40)
SCALE_TO = 10
WHH, STATE, W1S, W2S = range(4)
SEARCH_BITS = 3
SEARCH_PASSES = 10


def gru_moe(nc, x, x_t, cond_t, w_ih, w_hh, b_ih, b_hh, wg, bg, w1, w2, hs_rows, out):
    NB, T, D = x.shape
    N = NB * T
    E, _, H = w1.shape
    CAP = N // E
    L = T // SEG
    COLS = NB * SEG
    KD = D // P
    KH = H // P
    NT = N // P
    NG = CAP // P
    ROW = D + E
    GCOLS = 512
    NC_ = N // GCOLS
    STEPS_C = GCOLS // COLS
    NCAND = 2 ** SEARCH_BITS
    assert COLS == 64 and KD == 4 and BURN % 2 == 0 and BURN <= L and NG == 4 and E == 4

    with ExitStack() as ctx:
        def sb(name, shape, dt=F32):
            return ctx.enter_context(nc.sbuf_tensor(name, shape, dt))

        def sem(name):
            return ctx.enter_context(nc.semaphore(name))

        ps = ctx.enter_context(nc.psum_tensor("ps", [P, 8, 512], F32))

        big = sb("big", [P, 3 * KD * N])
        wa = sb("wa", [P, KD * H])
        wb = sb("wb", [P, KD * 3 * D])
        hx = sb("hx", [P, KD * N])

        gi = big[:, :].rearrange("p (j g c) -> p j g c", j=KD, g=3)
        w2_sb = big[:, 0:KH * D].rearrange("p (k d) -> p k d", k=KH)
        hid = big[:, KH * D:KH * D + KH * CAP].rearrange("p (k c) -> p k c", k=KH)
        rows0 = KH * (D + CAP)
        rows = big[:, rows0:rows0 + 8 * ROW].rearrange("p (n d) -> p n d", n=8)
        y = big[:, rows0:rows0 + NG * D].rearrange("p (g d) -> p g d", g=NG)
        later = [rows0 + 8 * ROW]

        def take(n):
            later[0] += n
            return big[:, later[0] - n:later[0]]
        tokrow = take(NG * ROW).rearrange("p (g d) -> p g d", g=NG)
        cmp4 = take(NT * E * E).rearrange("p (n e f) -> p n e f", n=NT, e=E)
        cmp5 = take(NT * E * E).rearrange("p (n e f) -> p n e f", n=NT, e=E)
        above = take(E * NCAND * NT).rearrange("p (e c n) -> p e c n", e=E, c=NCAND)
        wih_sb = wa[:, 0:KD * 3 * D].rearrange("p (k m) -> p k m", k=KD)
        w1_sb = wa[:, :].rearrange("p (k h) -> p k h", k=KD)
        whh_sb = wb[:, :].rearrange("p (k m) -> p k m", k=KD)
        whh_parts = wb[:, :].bitcast(F16).rearrange("p (k i m) -> p k i m", k=KD, i=2)
        spare = wa[:, KD * 3 * D:KD * 4 * D].bitcast(F16)
        parts_tmp = spare[:, 0:6 * D].rearrange("p (i m) -> p i m", i=2)
        slots = wb[:, 0:NT * CAP // 2].bitcast(F16).rearrange("p (n c) -> p n c", n=NT)
        tokT = wb[:, NT * CAP // 2:NT * CAP // 2 + KD * CAP].rearrange("p (k c) -> p k c", k=KD)
        xT = hx[:, :].rearrange("p (n k c) -> p n k c", n=NC_, k=KD)
        hsT = hx[:, :].rearrange("p (k c) -> p k c", k=KD)
        hsT_l = hx[:, :].rearrange("p (k c l) -> p k c l", k=KD, l=L)
        assert later[0] <= 3 * KD * N

        ident = sb("ident", [P, P])
        ones = sb("ones", [P, P])
        onesb = sb("onesb", [P, P], BF16)
        before = sb("before", [P, P], BF16)
        bih = sb("bih", [P, 12])
        bhh = sb("bhh", [P, 12])
        bsum = sb("bsum", [P, 12])
        h0 = sb("h0", [P, KD, NB])
        wg_sb = sb("wg_sb", [P, KD, E])
        bg_sb = sb("bg_sb", [P, E])
        state = sb("state", [P, 2, KD * COLS])
        start = sb("start", [P, KD * COLS])
        halves = sb("halves", [P, 2, KD, 2, COLS], F16)
        peak = sb("peak", [P, 4])
        peak_all = sb("peak_all", [P, 4])
        scale = sb("scale", [P, 4])
        unscale = sb("unscale", [P, 4])
        neg_sh = sb("neg_sh", [P, 1])
        un_gates = sb("un_gates", [P, 1])
        gates_scale = sb("gates_scale", [P, 1])
        bhn_s = sb("bhn_s", [P, KD])
        pre = sb("pre", [P, KD, 2, COLS])
        rz = sb("rz", [P, KD, 2, COLS])
        rn = sb("rn", [P, KD, COLS])
        cand_in = sb("cand_in", [P, KD, COLS])
        cand = sb("cand", [P, KD, COLS])
        zh = sb("zh", [P, KD, COLS])
        ocand = sb("ocand", [P, KD, COLS])
        dsq = sb("dsq", [P, KD * NB, SEG])
        hsq = sb("hsq", [P, KD * COLS])
        worst = sb("worst", [P, 4])
        flag = sb("flag", [P, SEG + 2], I32)
        lg = sb("lg", [P, NT, E])
        earlier = sb("earlier", [P, E, E])
        rank = sb("rank", [P, NT, E])
        lmax = sb("lmax", [P, NT])
        wsum = sb("wsum", [P, NT])
        prob = sb("prob", [P, NT, E])
        score = sb("score", [P, E, NT])
        steps_i = sb("steps_i", [P, SEARCH_PASSES, NCAND], I32)
        trial = sb("trial", [P, E, NCAND], I32)
        nabove = sb("nabove", [P, E, NCAND])
        keep = sb("keep", [P, E, NCAND])
        thr = sb("thr", [P, E])
        gt = sb("gt", [P, E, NT], BF16)
        eqp = sb("eqp", [P, E, 2 * NT], BF16)
        selp = sb("selp", [P, E, 2 * NT], BF16)
        fits = sb("fits", [P, E, NT], BF16)
        pos = sb("pos", [P, E, NT])
        slot_no = sb("slot_no", [P, CAP], F16)
        tok_id = sb("tok_id", [P, NT], F16)
        idx = sb("idx", [P, NG], I32)
        idx_out = sb("idx_out", [P, NG], I32)
        p_out = sb("p_out", [P, NG])

        state3 = [state[:, i, :].rearrange("p (k c) -> p k c", k=KD) for i in range(2)]
        state_s = state[:, 0, :].rearrange("p (kb s) -> p kb s", s=SEG)
        start_s = start[:, :].rearrange("p (kb s) -> p kb s", s=SEG)
        gate_ps = ps[:, 0:4, 0:3 * COLS].rearrange("p j (g c) -> p j g c", g=3)

        names = """small_loaded whh_loaded x_loaded out_init consts_pool consts_dve bias_ready
             gi_mm gi_ready peak_ready peak_known chain whh_ready zh_done high_ready h_ready gates_mm pre_ready sig_done rn_done
            candin_ready tanh_done ocand_done copied start_saved check_a worst_ready worst_mm flag_written flag_ready
            gru_over logits_mm turned rows_ready rows_copied rows_stored exp_in exp_done
            prob_ready nabove_ready total_mm masks_ready eq_mm sel_ready pos_mm pos_ready slots_ready list_mm idx_ready
            gathered tok_turned tokT_ready ffn1_mm hid_ready ffn2_mm y_ready scattered latched w1_loaded w2_loaded
            tables sp_waited pool_waited dve_waited pe_waited act_waited pool_consts""".split()
        S = {name: sem(name) for name in names}
        S["wih_loaded"] = [sem(f"wih_loaded_{g}") for g in range(3)]
        block = ctx.enter_context(nc.Block())

        whh_src = w_hh.rearrange("(k p) m -> p k m", p=P)
        wih_src = w_ih.rearrange("(k p) m -> p k m", p=P)
        w1_src = w1.rearrange("e (k p) h -> e p k h", p=P)
        w2_src = w2.rearrange("e (k p) d -> e p k d", p=P)
        rows_dst = hs_rows.rearrange("(n p) d -> n p d", p=P)

        HIGH, LOW = 0, 1
        EXACT = ((HIGH, HIGH), (HIGH, LOW), (LOW, HIGH))
        GUESS = ((HIGH, HIGH),)

        @block.sync
        def _(sp):
            sp.dma_start(xT[:, 0, :, :], x_t[:, 0, :, :]).then_inc(S["x_loaded"], 16)
            for g in range(3):
                sp.dma_start(wih_sb[:, :, g * D:(g + 1) * D], wih_src[:, :, g * D:(g + 1) * D]
                             ).then_inc(S["wih_loaded"][g], 16)
            for n in range(1, NC_):
                sp.wait_ge(S["x_loaded"], 16 * n)
                sp.dma_start(xT[:, n, :, :], x_t[:, n, :, :]).then_inc(S["x_loaded"], 16)
            for k in range(KD):
                sp.dma_start(whh_sb[:, k, :], whh_src[:, k, :]).then_inc(S["whh_loaded"], 16)
            sp.dma_start(out.rearrange("b t d -> (b t) d"), x.rearrange("b t d -> (b t) d")).then_inc(S["out_init"], 16)
            sp.wait_ge(S["gi_mm"], 12 * NC_)
            sp.wait_ge(S["whh_ready"], KD)
            for k in range(KD):
                sp.dma_start(w1_sb[:, k, :], w1_src[0, :, k, :]).then_inc(S["w1_loaded"], 16)
            sp.wait_ge(S["gru_over"], 1)
            for k in range(4):
                sp.dma_start(w2_sb[:, 4 * k:4 * k + 4, :], w2_src[0, :, 4 * k:4 * k + 4, :]).then_inc(S["w2_loaded"], 16)
            for n in range(NT):
                sp.wait_ge(S["rows_ready"], n + 1)
                if n == 0:
                    sp.wait_ge(S["prob_ready"], 1)
                sp.dma_start(rows_dst[n], rows[:, n % 8, :]).then_inc(S["rows_stored"], 16)
            with sp.Fori(1, E) as e:
                sp.wait_ge(S["ffn1_mm"], KH * e)
                sp.sem_inc(S["sp_waited"], 1)
                for k in range(KD):
                    sp.dma_start(w1_sb[:, k, :],
                                 w1_src[bass.ds(e, 1), :, k, :].rearrange("o p h -> (o p) h")).then_inc(S["w1_loaded"], 16)
                sp.wait_ge(S["ffn2_mm"], NG * e)
                sp.sem_inc(S["sp_waited"], 1)
                for k in range(4):
                    sp.dma_start(w2_sb[:, 4 * k:4 * k + 4, :],
                                 w2_src[bass.ds(e, 1), :, 4 * k:4 * k + 4, :].rearrange("o p k d -> (o p) k d")
                                 ).then_inc(S["w2_loaded"], 16)
            sp.wait_ge(S["out_init"], 16)
            sp.wait_ge(S["rows_stored"], 16 * NT)
            sp.wait_ge(S["scattered"], 16 * NG * E)

        @block.tensor
        def _(pe):
            pe.wait_ge(S["consts_pool"], 1)
            with pe.Fori(0, NC_) as c:
                pe.wait_ge(S["x_loaded"], c * 16 + 16)
                for m in range(12):
                    if m >= 2:
                        pe.wait_ge(S["gi_ready"], c * 12 + m - 1)
                    if m % 4 == 0:
                        pe.wait_ge(S["wih_loaded"][m // 4], 16)
                    for k in range(KD):
                        mm = pe.matmul(ps[:, 2 + m % 2, :], wih_sb[:, k, m * P:(m + 1) * P],
                                       xT[:, bass.ds(c, 1), k, :].rearrange("p o c -> p (o c)"), start=(k == 0), stop=(k == KD - 1))
                    mm.then_inc(S["gi_mm"], 1)
                pe.wait_ge(S["gi_ready"], c * 12 + 12)

            def gates(src, base, steps, products):
                have = [0]
                opened = set()

                def part(j, ks):
                    if j >= 2 and j not in opened:
                        pe.wait_ge(S["rn_done"], steps + j + 1)
                        opened.add(j)
                    for k in ks:
                        if k >= have[0]:
                            pe.wait_ge(S["h_ready"], base + k + 1)
                            have[0] = k + 1
                        for g in range(3):
                            for n, (w, h) in enumerate(products):
                                mm = pe.matmul(gate_ps[:, j, g, :], whh_parts[:, k, w, (4 * g + j) * P:(4 * g + j + 1) * P],
                                               halves[:, src, k, h, :], start=(k == 0 and g == 0 and n == 0),
                                               stop=(k == KD - 1 and n == len(products) - 1), skip_group_check=True)
                    if ks[-1] == KD - 1:
                        mm.then_inc(S["gates_mm"], 1)
                part(0, [0])
                part(0, [1])
                part(1, [0, 1])
                part(2, [0, 1])
                part(3, [0])
                part(0, [2])
                part(1, [2])
                part(0, [3])
                part(1, [3])
                part(2, [2, 3])
                part(3, [1, 2, 3])

            pe.wait_ge(S["whh_ready"], KD)
            with pe.Fori(0, BURN // 2) as i:
                for u in range(2):
                    gates(u, 8 * i + 4 * u, 8 * i + 4 * u, GUESS)
            with pe.Fori(0, SEG) as r:
                pe.wait_ge(S["flag_ready"], r + 1)
                pe.sem_inc(S["pe_waited"], 1)
                go = pe.value_load(flag[0:1, bass.ds(r, 1)])
                with pe.If(go > 0):
                    with pe.Fori(0, L // 2) as i:
                        for u in range(2):
                            gates(u, r * (4 * L + 4) + 8 * i + (4 * BURN + 4 + 4 * u),
                                  r * (4 * L) + 8 * i + (4 * BURN + 4 * u), EXACT)
                    pe.wait_ge(S["worst_ready"], r + 1)
                    pe.matmul(ps[0:1, 4, 0:1], worst[:, 2:3], ones[:, 0:1], start=True, stop=True).then_inc(S["worst_mm"], 1)

            pe.wait_ge(S["gru_over"], 1)
            pe.wait_ge(S["small_loaded"], 16 * 5)
            for n in range(NT):
                for k in range(KD):
                    mm = pe.matmul(ps[:, 5, n * E:(n + 1) * E], hsT[:, k, n * P:(n + 1) * P], wg_sb[:, k, :],
                                   start=(k == 0), stop=(k == KD - 1))
            mm.then_inc(S["logits_mm"], 1)
            for n in range(NT):
                if n >= 2:
                    pe.wait_ge(S["rows_copied"], n - 1)
                for k in range(KD):
                    mm = pe.transpose(ps[:, n % 2, k * P:(k + 1) * P], hsT[:, k, n * P:(n + 1) * P], ident[:, :])
                mm.then_inc(S["turned"], 1)
            with pe.Fori(0, SEARCH_PASSES) as i:
                pe.wait_ge(S["nabove_ready"], i + 1)
                pe.matmul(ps[:, 6, 0:E * NCAND], ones[:, :], nabove[:, :, :].rearrange("p e c -> p (e c)"),
                          start=True, stop=True).then_inc(S["total_mm"], 1)

            def earlier_count(bank, maskp, more):
                o = ps[:, bank, 0:E * NT].rearrange("p (e n) -> p e n", e=E)
                pe.matmul(o, before[:, :], maskp[:, :, NT:2 * NT], start=True, stop=False)
                for d in range(1, NT):
                    mm = pe.matmul(o, onesb[:, :], maskp[:, :, NT - d:2 * NT - d], start=False,
                                   stop=(d == NT - 1 and not more))
                if more:
                    for n in range(NT):
                        mm = pe.matmul(o, onesb[:, :], gt[:, :, n:n + 1].to_broadcast([P, E, NT]), start=False,
                                       stop=(n == NT - 1))
                return mm

            pe.wait_ge(S["masks_ready"], 1)
            earlier_count(7, eqp, True).then_inc(S["eq_mm"], 1)
            pe.wait_ge(S["sel_ready"], 1)
            earlier_count(7, selp, False).then_inc(S["pos_mm"], 1)

            def token_list(e):
                pe.wait_ge(S["slots_ready"], NT * e + NT)
                for n in range(NT):
                    for g in range(NG):
                        mm = pe.matmul(ps[:, 6, g:g + 1], slots[:, n, g * P:(g + 1) * P], tok_id[:, n:n + 1],
                                       start=(n == 0 and g == 0), stop=(n == NT - 1), skip_group_check=True)
                mm.then_inc(S["list_mm"], 1)

            def turn_tokens(e):
                pe.wait_ge(S["gathered"], 16 * NG * e + 16 * NG)
                for g in range(NG):
                    if g >= 2:
                        pe.wait_ge(S["tokT_ready"], NG * e + g - 1)
                    for k in range(KD):
                        mm = pe.transpose(ps[:, 4 + g % 2, k * P:(k + 1) * P], tokrow[:, g, k * P:(k + 1) * P],
                                          ident[:, :])
                    mm.then_inc(S["tok_turned"], 1)

            def expert(e, last):
                pe.wait_ge(S["tokT_ready"], NG * e + NG)
                pe.wait_ge(S["w1_loaded"], 16 * KD * e + 16 * KD)
                for m in range(KH):
                    if m >= 2:
                        pe.wait_ge(S["hid_ready"], KH * e + m - 1)
                    for k in range(KD):
                        mm = pe.matmul(ps[:, m % 2, :], w1_sb[:, k, m * P:(m + 1) * P], tokT[:, k, :],
                                       start=(k == 0), stop=(k == KD - 1))
                    mm.then_inc(S["ffn1_mm"], 1)
                if not last:
                    token_list(e + 1)
                pe.wait_ge(S["hid_ready"], KH * e + KH)
                pe.wait_ge(S["w2_loaded"], 64 * e + 64)
                for g in range(NG):
                    if g >= 2:
                        pe.wait_ge(S["y_ready"], NG * e + g - 1)
                    for k in range(KH):
                        mm = pe.matmul(ps[:, 2 + g % 2, :], hid[:, k, g * P:(g + 1) * P], w2_sb[:, k, :],
                                       start=(k == 0), stop=(k == KH - 1))
                    mm.then_inc(S["ffn2_mm"], 1)
                    if g == 1 and not last:
                        turn_tokens(e + 1)
                pe.wait_ge(S["y_ready"], NG * e + NG)

            token_list(0)
            turn_tokens(0)
            with pe.Fori(0, E - 1) as e:
                expert(e, False)
            expert(E - 1, True)

        @block.scalar
        def _(act):
            act.dma_start(bih[:, :], b_ih).then_inc(S["small_loaded"], 16)
            act.dma_start(bhh[:, :], b_hh).then_inc(S["small_loaded"], 16)
            act.dma_start(h0[:, :, :], cond_t).then_inc(S["small_loaded"], 16)
            act.dma_start(wg_sb[:, :, :], wg).then_inc(S["small_loaded"], 16)
            act.dma_start(bg_sb[:, :], bg.rearrange("(o e) -> o e", o=1).to_broadcast([P, E])).then_inc(S["small_loaded"], 16)
            act.wait_ge(S["consts_dve"], 1)
            act.activation(cand[:, 0, 0:1], ones[:, 0:1], ACT.Sigmoid).then_inc(S["tables"], 1)
            act.wait_ge(S["tables"], 1)

            act.wait_ge(S["bias_ready"], 1)
            with act.Fori(0, NC_) as c:
                for m in range(12):
                    act.wait_ge(S["gi_mm"], c * 12 + m + 1)
                    act.activation(gi[:, m % 4, m // 4, bass.ds(c * GCOLS, GCOLS)], ps[:, 2 + m % 2, :], ACT.Identity,
                                   bias=bsum[:, m:m + 1]).then_inc(S["gi_ready"], 1)

            def step(base):
                def sig(j):
                    act.wait_ge(S["pre_ready"], base + j + 1)
                    act.activation(rz[:, j, :, :], pre[:, j, :, :], ACT.Sigmoid).then_inc(S["sig_done"], 1)

                def tanh(j):
                    act.wait_ge(S["candin_ready"], base + j + 1)
                    act.activation(cand[:, j, :], cand_in[:, j, :], ACT.Tanh).then_inc(S["tanh_done"], 1)
                for f, j in ((sig, 0), (sig, 1), (tanh, 0), (tanh, 1), (sig, 2), (tanh, 2), (sig, 3), (tanh, 3)):
                    f(j)

            with act.Fori(0, BURN // 2) as i:
                for u in range(2):
                    step(8 * i + 4 * u)
            with act.Fori(0, SEG) as r:
                act.wait_ge(S["flag_ready"], r + 1)
                act.sem_inc(S["act_waited"], 1)
                go = act.value_load(flag[0:1, bass.ds(r, 1)])
                with act.If(go > 0):
                    with act.Fori(0, L // 2) as i:
                        for u in range(2):
                            step(4 * L * r + 8 * i + (4 * BURN + 4 * u))

            for n in range(NT):
                act.wait_ge(S["turned"], n + 1)
                if n == 0:
                    act.wait_ge(S["gru_over"], 1)
                if n >= 8:
                    act.wait_ge(S["rows_stored"], 16 * NT // 2)
                act.copy(rows[:, n % 8, 0:D], ps[:, n % 2, :]).then_inc(S["rows_copied"], 1)
                if n == 3:
                    act.wait_ge(S["exp_in"], 1)
                    act.activation(prob[:, :, :], lg[:, :, :], ACT.Exp).then_inc(S["exp_done"], 1)

            def gelu(e):
                for m in range(KH):
                    act.wait_ge(S["ffn1_mm"], KH * e + m + 1)
                    act.activation(hid[:, m, :], ps[:, m % 2, :], ACT.Gelu).then_inc(S["hid_ready"], 1)
            with act.Fori(0, E) as e:
                gelu(e)

        @block.gpsimd
        def _(pool):
            pool.memset(ident[:, :], 0.0).then_inc(S["pool_consts"], 1)
            pool.wait_ge(S["pool_consts"], 1)
            pool.affine_select(out=ident[:, :], in_=ident[:, :], compare_op=ALU.not_equal, fill=1.0, base=0,
                               pattern=[[-1, P]], channel_multiplier=1).then_inc(S["consts_pool"], 1)
            pool.memset(before[:, :], 0.0).then_inc(S["pool_consts"], 1)
            pool.wait_ge(S["pool_consts"], 2)
            pool.affine_select(out=before[:, :], in_=before[:, :], compare_op=ALU.is_ge, fill=1.0, base=0,
                               pattern=[[-1, P]], channel_multiplier=1).then_inc(S["consts_pool"], 1)
            pool.iota(slot_no[:, :], [[1, CAP]], base=0, channel_multiplier=0,
                      allow_small_or_imprecise_dtypes=True).then_inc(S["consts_pool"], 1)
            pool.iota(tok_id[:, :], [[P, NT]], base=0, channel_multiplier=1,
                      allow_small_or_imprecise_dtypes=True).then_inc(S["consts_pool"], 1)
            pool.memset(earlier[:, :, :], 0.0).then_inc(S["pool_consts"], 1)
            pool.wait_ge(S["pool_consts"], 3)
            pool.affine_select(out=earlier[:, :, :], in_=earlier[:, :, :], compare_op=ALU.is_ge, fill=1.0, base=0,
                               pattern=[[-1, E], [1, E]], channel_multiplier=0).then_inc(S["consts_pool"], 1)
            pool.wait_ge(S["peak_ready"], 1)
            pool.partition_all_reduce(peak_all[:, 0:2], peak[:, 0:2], P, RMAX).then_inc(S["peak_known"], 1)
            pool.memset(worst[:, 3:4], 0.0).then_inc(S["copied"], 2)

            def carry(src, base):
                for j in range(KD):
                    pool.wait_ge(S["sig_done"], base + j + 1)
                    pool.tensor_tensor(zh[:, j, :], rz[:, j, 1, :], state3[src][:, j, :], ALU.mult
                                       ).then_inc(S["zh_done"], 1)

            with pool.Fori(0, BURN // 2) as i:
                for u in range(2):
                    carry(u, 8 * i + 4 * u)
            with pool.Fori(0, SEG) as r:
                pool.wait_ge(S["flag_ready"], r + 1)
                pool.sem_inc(S["pool_waited"], 1)
                go = pool.value_load(flag[0:1, bass.ds(r, 1)])
                with pool.If(go > 0):
                    with pool.Fori(0, L // 2) as i:
                        for u in range(2):
                            carry(u, 4 * L * r + 8 * i + (4 * BURN + 4 * u))
                            pool.wait_ge(S["h_ready"], r * (4 * L + 4) + 8 * i + (4 * BURN + 12 + 4 * u))
                            pool.tensor_copy(
                                hsT_l[:, :, :, bass.ds(2 * i + u, 1)].rearrange("p k c o -> p k (c o)"),
                                state3[1 - u]).then_inc(S["copied"], 1)

            def gather(e):
                pool.wait_ge(S["idx_ready"], e + 1)
                pool.sem_inc(S["pool_waited"], 1)
                for g in range(NG):
                    pool.indirect_dma_start(
                        out=tokrow[:, g, :], out_offset=None, in_=hs_rows,
                        in_offset=bass.IndirectOffsetOnAxis(ap=idx[:, g:g + 1], axis=0)).then_inc(S["gathered"], 16)

            def scatter(e):
                for g in range(NG):
                    pool.wait_ge(S["y_ready"], NG * e + g + 1)
                    pool.sem_inc(S["pool_waited"], 1)
                    pool.indirect_dma_start(
                        out=out.rearrange("b t d -> (b t) d"),
                        out_offset=bass.IndirectOffsetOnAxis(ap=idx_out[:, g:g + 1], axis=0),
                        in_=y[:, g, :], in_offset=None, compute_op=ALU.add).then_inc(S["scattered"], 16)

            pool.wait_ge(S["rows_stored"], 16 * NT)
            pool.wait_ge(S["out_init"], 16)
            gather(0)
            with pool.Fori(0, E - 1) as e:
                pool.wait_ge(S["latched"], e + 1)
                pool.sem_inc(S["pool_waited"], 1)
                gather(e + 1)
                scatter(e)
            scatter(E - 1)

        @block.vector
        def _(dve):
            dve.memset(ones[:, :], 1.0).then_inc(S["consts_dve"], 1)
            dve.memset(onesb[:, :], 1.0)
            dve.memset(flag[:, :], 0)
            dve.memset(eqp[:, :, 0:NT], 0.0)
            dve.memset(selp[:, :, 0:NT], 0.0)
            dve.memset(state[:, 0, :], 0.0).then_inc(S["rn_done"], KD)
            dve.memset(halves[:, 0, :, :, :], 0.0).then_inc(S["h_ready"], 4)
            dve.wait_ge(S["small_loaded"], 16 * 5)
            dve.tensor_tensor(bsum[:, 0:8], bih[:, 0:8], bhh[:, 0:8], ALU.add)
            dve.tensor_copy(bsum[:, 8:12], bih[:, 8:12]).then_inc(S["bias_ready"], 1)
            dve.wait_ge(S["bias_ready"], 1)

            link_n = [0]

            def link(ins):
                link_n[0] += 1
                ins.then_inc(S["chain"], 1)
                dve.wait_ge(S["chain"], link_n[0])

            def pow2(cols):
                link(dve.tensor_scalar(peak_all[:, cols], peak_all[:, cols], 1e-30, None, ALU.max))
                link(dve.tensor_scalar(unscale[:, cols].bitcast(I32), peak_all[:, cols].bitcast(I32), 0x7F800000, None,
                                       ALU.bitwise_and))
                dve.tensor_scalar(scale[:, cols].bitcast(I32), unscale[:, cols].bitcast(I32), -1.0,
                                  float((254 + SCALE_TO) << 23), ALU.mult, ALU.add)
                link(dve.tensor_scalar(unscale[:, cols].bitcast(I32), unscale[:, cols].bitcast(I32),
                                       -float(SCALE_TO << 23), None, ALU.add))

            dve.tensor_reduce(peak[:, STATE:STATE + 1], h0[:, :, :], AX.XY, ALU.max, apply_absolute_value=True)
            dve.wait_ge(S["whh_loaded"], 16 * KD)
            link(dve.tensor_reduce(peak[:, WHH:WHH + 1], whh_sb, AX.XY, ALU.max, apply_absolute_value=True))
            link(dve.tensor_scalar(peak[:, STATE:STATE + 1], peak[:, STATE:STATE + 1], 1.0, None, ALU.max))
            dve.sem_inc(S["peak_ready"], 1)
            dve.wait_ge(S["peak_known"], 1)
            pow2(slice(WHH, STATE + 1))
            dve.tensor_scalar(neg_sh[:, :], scale[:, STATE:STATE + 1], -1.0, None, ALU.mult)
            dve.tensor_tensor(un_gates[:, :], unscale[:, WHH:WHH + 1], unscale[:, STATE:STATE + 1], ALU.mult)
            dve.tensor_scalar(h0[:, :, :], h0[:, :, :], scale[:, STATE:STATE + 1], None, ALU.mult)
            link(dve.tensor_tensor(gates_scale[:, :], scale[:, WHH:WHH + 1], scale[:, STATE:STATE + 1], ALU.mult))
            link(dve.tensor_scalar(bhn_s[:, :], bhh[:, 8:12], gates_scale[:, 0:1], None, ALU.mult))
            for k in range(KD):
                link(dve.tensor_scalar(parts_tmp[:, HIGH, :], whh_sb[:, k, :], scale[:, WHH:WHH + 1], None, ALU.mult))
                link(dve.scalar_tensor_tensor(parts_tmp[:, LOW, :], whh_sb[:, k, :], scale[:, WHH:WHH + 1],
                                              parts_tmp[:, HIGH, :], ALU.mult, ALU.subtract))
                link(dve.tensor_copy(whh_parts[:, k, :, :], parts_tmp[:, :, :]))
                dve.sem_inc(S["whh_ready"], 1)
            dve.wait_ge(S["gi_ready"], 12 * NC_)

            def split(dst, k0, k1):
                dve.tensor_tensor(halves[:, dst, k0:k1, LOW, :], state3[dst][:, k0:k1, :],
                                  halves[:, dst, k0:k1, HIGH, :], ALU.subtract).then_inc(S["h_ready"], k1 - k0)

            def step(src, l, base, wait_copy):
                col = l * COLS
                dst = 1 - src

                def pre_rz(j):
                    dve.wait_ge(S["gates_mm"], base + j + 1)
                    dve.scalar_tensor_tensor(pre[:, j, :, :], gate_ps[:, j, 0:2, :], un_gates[:, 0:1],
                                             gi[:, j, 0:2, bass.ds(col, COLS)], ALU.mult, ALU.add
                                             ).then_inc(S["pre_ready"], 1)

                def candidate_in(j):
                    dve.wait_ge(S["sig_done"], base + j + 1)
                    dve.scalar_tensor_tensor(rn[:, j, :], gate_ps[:, j, 2, :], bhn_s[:, j:j + 1], rz[:, j, 0, :],
                                             ALU.add, ALU.mult).then_inc(S["rn_done"], 1)
                    dve.wait_ge(S["rn_done"], base + (KD + j + 1))
                    dve.scalar_tensor_tensor(cand_in[:, j, :], rn[:, j, :], un_gates[:, 0:1],
                                             gi[:, j, 2, bass.ds(col, COLS)], ALU.mult, ALU.add
                                             ).then_inc(S["candin_ready"], 1)

                def blend(j):
                    dve.wait_ge(S["tanh_done"], base + j + 1)
                    dve.scalar_tensor_tensor(ocand[:, j, :], rz[:, j, 1, :], -1.0, cand[:, j, :],
                                             ALU.add, ALU.mult).then_inc(S["ocand_done"], 1)
                    if j == 0 and wait_copy is not None:
                        dve.wait_ge(S["copied"], wait_copy)
                    dve.wait_ge(S["zh_done"], base + j + 1)
                    dve.wait_ge(S["ocand_done"], base + j + 1)
                    dve.scalar_tensor_tensor(halves[:, dst, j, HIGH, :], ocand[:, j, :], neg_sh[:, 0:1], zh[:, j, :],
                                             ALU.mult, ALU.add)
                    dve.scalar_tensor_tensor(state3[dst][:, j, :], ocand[:, j, :], neg_sh[:, 0:1], zh[:, j, :],
                                             ALU.mult, ALU.add).then_inc(S["high_ready"], 1)
                    dve.wait_ge(S["high_ready"], base + j + 1)
                    split(dst, j, j + 1)
                pre_rz(0)
                pre_rz(1)
                candidate_in(0)
                candidate_in(1)
                blend(0)
                blend(1)
                pre_rz(2)
                candidate_in(2)
                pre_rz(3)
                blend(2)
                candidate_in(3)
                blend(3)

            def next_start(count):
                dve.tensor_copy(start_s[:, :, 1:SEG], state_s[:, :, 0:SEG - 1]).then_inc(S["start_saved"], 1)
                dve.wait_ge(S["start_saved"], 2 * count - 1)
                dve.tensor_copy(state[:, 0, :], start[:, :])
                dve.tensor_copy(halves[:, 0, :, HIGH, :], start[:, :].rearrange("p (k c) -> p k c", k=KD)
                                ).then_inc(S["start_saved"], 1)
                dve.wait_ge(S["start_saved"], 2 * count)
                split(0, 0, KD)

            with dve.Fori(0, BURN // 2) as i:
                for u in range(2):
                    step(u, 2 * i + (L - BURN + u), 8 * i + 4 * u, None)
            dve.wait_ge(S["h_ready"], 4 * BURN + 4)
            dve.tensor_copy(start_s[:, :, 0:1], h0[:, :, :].rearrange("p k b -> p (k b)").unsqueeze(2))
            next_start(1)
            dve.memset(flag[:, 0:1], 1).then_inc(S["flag_written"], 1)
            dve.wait_ge(S["flag_written"], 1)
            dve.sem_inc(S["flag_ready"], 1)

            with dve.Fori(0, SEG) as r:
                dve.wait_ge(S["flag_ready"], r + 1)
                dve.sem_inc(S["dve_waited"], 1)
                go = dve.value_load(flag[0:1, bass.ds(r, 1)])
                with dve.If(go > 0):
                    with dve.Fori(0, L // 2) as i:
                        for u in range(2):
                            step(u, 2 * i + u, 4 * L * r + 8 * i + (4 * BURN + 4 * u), L * r + 2 * i + (u + 1))
                    dve.wait_ge(S["h_ready"], r * (4 * L + 4) + (4 * BURN + 8 + 4 * L))
                    dve.tensor_tensor(dsq[:, :, 0:SEG - 1], state_s[:, :, 0:SEG - 1], start_s[:, :, 1:SEG],
                                      ALU.subtract).then_inc(S["check_a"], 1)
                    dve.tensor_tensor(hsq[:, :], state[:, 0, :], state[:, 0, :], ALU.mult).then_inc(S["check_a"], 1)
                    dve.wait_ge(S["check_a"], 6 * r + 2)
                    dve.tensor_tensor(dsq[:, :, 0:SEG - 1], dsq[:, :, 0:SEG - 1], dsq[:, :, 0:SEG - 1],
                                      ALU.mult).then_inc(S["check_a"], 1)
                    dve.tensor_reduce(worst[:, 1:2], hsq[:, :], AX.X, ALU.max).then_inc(S["check_a"], 1)
                    dve.wait_ge(S["check_a"], 6 * r + 4)
                    dve.tensor_reduce(worst[:, 0:1], dsq[:, :, 0:SEG - 1], AX.XY, ALU.max).then_inc(S["check_a"], 1)
                    dve.wait_ge(S["check_a"], 6 * r + 5)
                    dve.scalar_tensor_tensor(worst[:, 2:3], worst[:, 1:2], TOL2, worst[:, 0:1],
                                             ALU.mult, ALU.is_lt).then_inc(S["worst_ready"], 1)
                    dve.wait_ge(S["copied"], L * r + (L + 2))
                    next_start(r + 2)
                    dve.wait_ge(S["worst_mm"], r + 1)
                    dve.tensor_copy(flag[0:1, bass.ds(r + 1, 1)], ps[0:1, 4, 0:1]).then_inc(S["check_a"], 1)
                    dve.wait_ge(S["check_a"], 6 * r + 6)
                    dve.sem_inc(S["flag_written"], 1)
                dve.sem_inc(S["flag_ready"], 1)
            dve.sem_inc(S["gru_over"], 1)

            dve.wait_ge(S["consts_pool"], 5)
            dve.wait_ge(S["logits_mm"], 1)
            lgp = ps[:, 5, 0:NT * E].rearrange("p (n e) -> p n e", n=NT)
            mine = lg[:, :, :].unsqueeze(3).to_broadcast([P, NT, E, E])
            other = lg[:, :, :].unsqueeze(2).to_broadcast([P, NT, E, E])
            link(dve.scalar_tensor_tensor(lg[:, :, :], lgp, unscale[:, STATE:STATE + 1], bg_sb[:, :].unsqueeze(1).to_broadcast([P, NT, E]), ALU.mult, ALU.add))
            dve.tensor_tensor(cmp4[:, :, :, :], other, mine, ALU.is_gt)
            dve.tensor_tensor(cmp5[:, :, :, :], other, mine, ALU.is_equal)
            link(dve.tensor_reduce(lmax[:, :], lg[:, :, :], AX.X, ALU.max))
            link(dve.tensor_tensor(cmp5[:, :, :, :], cmp5[:, :, :, :],
                                   earlier[:, :, :].unsqueeze(1).to_broadcast([P, NT, E, E]), ALU.mult))
            dve.tensor_tensor(lg[:, :, :], lg[:, :, :], lmax[:, :].unsqueeze(2).to_broadcast([P, NT, E]),
                              ALU.subtract).then_inc(S["exp_in"], 1)
            link(dve.tensor_tensor(cmp4[:, :, :, :], cmp4[:, :, :, :], cmp5[:, :, :, :], ALU.add))
            link(dve.tensor_reduce(rank[:, :, :], cmp4[:, :, :, :], AX.X, ALU.add))
            dve.wait_ge(S["exp_done"], 1)
            link(dve.scalar_tensor_tensor(prob[:, :, :], rank[:, :, :], 2.0, prob[:, :, :], ALU.is_lt, ALU.mult))
            link(dve.tensor_reduce(wsum[:, :], prob[:, :, :], AX.X, ALU.add))
            link(dve.reciprocal(wsum[:, :], wsum[:, :]))
            link(dve.tensor_tensor(prob[:, :, :], prob[:, :, :], wsum[:, :].unsqueeze(2).to_broadcast([P, NT, E]),
                                   ALU.mult))
            dve.tensor_copy(score[:, :, :], prob[:, :, :].rearrange("p n e -> p e n"))
            link(dve.memset(thr[:, :], 0.0))
            for n in range(NT):
                dve.wait_ge(S["rows_copied"], n + 1)
                ins = dve.tensor_copy(rows[:, n % 8, D:ROW], prob[:, n, :])
                ins.then_inc(S["rows_ready"], 1)
                if n == 0:
                    dve.sem_inc(S["prob_ready"], 1)

            for i in range(SEARCH_PASSES):
                shift = SEARCH_BITS * (SEARCH_PASSES - 1 - i)
                for c in range(NCAND):
                    ins = dve.memset(steps_i[:, i, c:c + 1], c << shift)
            link(ins)
            with dve.Fori(0, SEARCH_PASSES) as i:
                base = link_n[0]
                dve.tensor_tensor(trial[:, :, :], thr[:, :].bitcast(I32).unsqueeze(2).to_broadcast([P, E, NCAND]),
                                  steps_i[:, bass.ds(i, 1), :].to_broadcast([P, E, NCAND]),
                                  ALU.bitwise_or).then_inc(S["chain"], 1)
                dve.wait_ge(S["chain"], 4 * i + (base + 1))
                dve.tensor_tensor(above[:, :, :, :], score[:, :, :].unsqueeze(2).to_broadcast([P, E, NCAND, NT]),
                                  trial[:, :, :].bitcast(F32).unsqueeze(3).to_broadcast([P, E, NCAND, NT]),
                                  ALU.is_ge).then_inc(S["chain"], 1)
                dve.wait_ge(S["chain"], 4 * i + (base + 2))
                dve.tensor_reduce(nabove[:, :, :], above[:, :, :, :], AX.X, ALU.add).then_inc(S["nabove_ready"], 1)
                dve.wait_ge(S["total_mm"], i + 1)
                dve.scalar_tensor_tensor(keep[:, :, :], ps[:, 6, 0:E * NCAND].rearrange("p (e c) -> p e c", e=E),
                                         float(CAP), trial[:, :, :].bitcast(F32), ALU.is_ge,
                                         ALU.mult).then_inc(S["chain"], 1)
                dve.wait_ge(S["chain"], 4 * i + (base + 3))
                dve.tensor_reduce(thr[:, :], keep[:, :, :], AX.X, ALU.max).then_inc(S["chain"], 1)
                dve.wait_ge(S["chain"], 4 * i + (base + 4))
            link_n[0] += 4 * SEARCH_PASSES

            thr_b = thr[:, :].unsqueeze(2).to_broadcast([P, E, NT])
            ps7 = ps[:, 7, 0:E * NT].rearrange("p (e n) -> p e n", e=E)
            dve.tensor_tensor(gt[:, :, :], score[:, :, :], thr_b, ALU.is_gt)
            link(dve.tensor_tensor(eqp[:, :, NT:2 * NT], score[:, :, :], thr_b, ALU.is_equal))
            dve.sem_inc(S["masks_ready"], 1)
            dve.wait_ge(S["eq_mm"], 1)
            link(dve.scalar_tensor_tensor(fits[:, :, :], ps7, float(CAP), eqp[:, :, NT:2 * NT], ALU.is_lt, ALU.mult))
            link(dve.tensor_tensor(selp[:, :, NT:2 * NT], fits[:, :, :], gt[:, :, :], ALU.add))
            dve.sem_inc(S["sel_ready"], 1)
            dve.wait_ge(S["pos_mm"], 1)
            link(dve.scalar_tensor_tensor(pos[:, :, :], ps7, 1.0, selp[:, :, NT:2 * NT], ALU.add, ALU.mult))
            link(dve.tensor_scalar(pos[:, :, :], pos[:, :, :], -1.0, None, ALU.add))

            def one_hot(e):
                for n in range(NT):
                    dve.tensor_scalar(slots[:, n, :], slot_no[:, :], pos[:, bass.ds(e, 1), n:n + 1].rearrange("p o n -> p (o n)"),
                                      None, ALU.is_equal).then_inc(S["slots_ready"], 1)

            def make_idx(e):
                dve.wait_ge(S["list_mm"], e + 1)
                dve.tensor_copy(idx[:, :], ps[:, 6, 0:NG]).then_inc(S["idx_ready"], 1)

            def tokens_T(e):
                for g in range(NG):
                    dve.wait_ge(S["tok_turned"], NG * e + g + 1)
                    dve.tensor_scalar(tokT[:, :, g * P:(g + 1) * P],
                                    ps[:, 4 + g % 2, :].rearrange("p (k c) -> p k c", k=KD), unscale[:, STATE:STATE+1], None, ALU.mult).then_inc(S["tokT_ready"], 1)

            def latch(e):
                dve.tensor_copy(idx_out[:, :], idx[:, :])
                dve.tensor_copy(p_out[:, :], tokrow[:, :, bass.ds(D + e, 1)].rearrange("p g o -> p (g o)")
                                ).then_inc(S["latched"], 1)
                dve.wait_ge(S["latched"], e + 1)

            def weigh(e, g):
                dve.wait_ge(S["ffn2_mm"], NG * e + g + 1)
                dve.tensor_scalar(y[:, g, :], ps[:, 2 + g % 2, :], p_out[:, g:g + 1], None,
                                  ALU.mult).then_inc(S["y_ready"], 1)

            one_hot(0)
            make_idx(0)
            tokens_T(0)
            latch(0)
            with dve.Fori(0, E - 1) as e:
                one_hot(e + 1)
                make_idx(e + 1)
                weigh(e, 0)
                weigh(e, 1)
                tokens_T(e + 1)
                weigh(e, 2)
                weigh(e, 3)
                dve.wait_ge(S["scattered"], 16 * NG * e + 16 * NG)
                latch(e + 1)
            for g in range(NG):
                weigh(E - 1, g)


def laid_out(inputs):
    x = np.asarray(inputs['x'])
    nb, t, d = x.shape
    kd, steps = d // P, t // SEG
    x_t = x.reshape(nb * SEG, steps, kd, P).transpose(3, 2, 1, 0).reshape(P, kd, -1, 512).transpose(0, 2, 1, 3)
    return {
        'x': x,
        'x_t': x_t,
        'cond_t': np.asarray(inputs['cond_2048']).reshape(nb, kd, P).transpose(2, 1, 0),
        'w_ih': inputs['L0_cond_W_ih'],
        'w_hh': inputs['L0_cond_W_hh'],
        'b_ih': np.asarray(inputs['L0_cond_b_ih']).reshape(-1, P).T,
        'b_hh': np.asarray(inputs['L0_cond_b_hh']).reshape(-1, P).T,
        'wg': np.asarray(inputs['L0_ffn_Wg']).reshape(kd, P, -1).transpose(1, 0, 2),
        'bg': inputs['L0_ffn_bg'],
        'w1': inputs['L0_ffn_W1'],
        'w2': inputs['L0_ffn_W2'],
    }


def kernel(**inputs):
    import concourse.bacc as bacc
    from concourse.bass_utils import run_bass_kernel_spmd

    nc = bacc.Bacc("TRN2", target_bir_lowering=False, num_devices=1)
    arrays, args = {}, []
    for name, a in laid_out(inputs).items():
        a = np.ascontiguousarray(a)
        arrays[f"in_{name}"] = a
        args.append(nc.dram_tensor(f"in_{name}", a.shape, mybir.dt.from_np(a.dtype), kind="ExternalInput").ap())
    shape = inputs['x'].shape
    experts = inputs['L0_ffn_Wg'].shape[1]
    hs_rows = nc.dram_tensor("hs_rows", (shape[0] * shape[1], shape[2] + experts), F32, kind="Internal").ap()
    out = nc.dram_tensor("out_0", shape, F32, kind="ExternalOutput").ap()
    gru_moe(nc, *args, hs_rows, out)
    r = run_bass_kernel_spmd(nc, [arrays], core_ids=[0])
    return r.results[0]["out_0"]
```

```python
from contextlib import ExitStack

import numpy as np
import concourse.bass as bass
from concourse import mybir

ALU = mybir.AluOpType
ACT = mybir.ActivationFunctionType
AX = mybir.AxisListType
RMAX = bass.bass_isa.ReduceOp.max
F32 = mybir.dt.float32
F16 = mybir.dt.float16
BF16 = mybir.dt.bfloat16
I32 = mybir.dt.int32

P = 128
SEG = 16
BURN = 8
ROUGH = 8
TOL = float(2.0 ** -20)
SCALE_TO = 10
HIDDEN_TO = float(2.0 ** -16)
WHH, STATE, W1, W2, WIH, X = range(6)
SEARCH_BITS = 3
SEARCH_PASSES = 10


def gru_moe(nc, x, x_t, cond_t, w_ih, w_hh, b_ih, b_hh, wg, bg, w1, w2, hs_rows, out):
    NB, T, D = x.shape
    N = NB * T
    E, _, H = w1.shape
    CAP = N // E
    L = T // SEG
    COLS = NB * SEG
    KD = D // P
    KH = H // P
    NT = N // P
    NG = CAP // P
    ROW = D + E
    GCOLS = 512
    NC_ = N // GCOLS
    NCAND = 2 ** SEARCH_BITS
    assert 2 * COLS == P and KD == 4 and BURN % 2 == 0 and ROUGH % 2 == 0 and L % 2 == 0 and NG == 4 and E == 4

    with ExitStack() as ctx:
        def sb(name, shape, dt=F32):
            return ctx.enter_context(nc.sbuf_tensor(name, shape, dt))

        def sem(name):
            return ctx.enter_context(nc.semaphore(name))

        ps = ctx.enter_context(nc.psum_tensor("ps", [P, 8, 512], F32))

        big = sb("big", [P, 3 * KD * N])
        wa = sb("wa", [P, KD * H])
        wb = sb("wb", [P, KD * 3 * D])
        hx = sb("hx", [P, (L + 1) * KD * COLS])

        gi = big[:, :].rearrange("p (j g c) -> p j g c", j=KD, g=3)
        WM = KD * H
        w_parts = {W1: big[:, 0:WM].bitcast(F16).rearrange("p (i m) -> p i m", i=2),
                   W2: big[:, WM:2 * WM].bitcast(F16).rearrange("p (i m) -> p i m", i=2)}
        w1p = w_parts[W1].rearrange("p i (k h) -> p i k h", k=KD)
        w2p = w_parts[W2].rearrange("p i (k d) -> p i k d", k=KH)
        hid = big[:, 2 * WM:3 * WM].bitcast(F16).rearrange("p (i k c) -> p i k c", i=2, k=KH)
        later = [WM]

        def take(n):
            later[0] += n
            return big[:, later[0] - n:later[0]]
        rows = take(NT * ROW).rearrange("p (n d) -> p n d", n=NT)
        cmp4 = take(NT * E * E).rearrange("p (n e f) -> p n e f", n=NT, e=E)
        cmp5 = take(NT * E * E).rearrange("p (n e f) -> p n e f", n=NT, e=E)
        above = take(E * NCAND * NT // 2).bitcast(BF16).rearrange("p (n e c) -> p n e c", e=E, c=NCAND)
        wih_sb = wa[:, 0:KD * 3 * D].rearrange("p (k m) -> p k m", k=KD)
        stage = wa[:, :]
        CHUNKS, CHUNK = 4, WM // 4
        whh_sb = wa[:, 0:KD * 3 * D].rearrange("p (k m) -> p k m", k=KD)
        whh_parts = wa[:, 0:KD * 3 * D].bitcast(F16).rearrange("p (k i m) -> p k i m", k=KD, i=2)
        spare = wa[:, KD * 3 * D:KD * 4 * D].bitcast(F16)
        parts_tmp = spare[:, 0:6 * D].rearrange("p (i m) -> p i m", i=2)
        slots = wb[:, 0:NT * CAP // 2].bitcast(F16).rearrange("p (n c) -> p n c", n=NT)
        tokT = wb[:, NT * CAP // 2:NT * CAP // 2 + KD * CAP].bitcast(F16).rearrange("p (i k c) -> p i k c", i=2, k=KD)
        wih_parts = wb[:, :].bitcast(F16).rearrange("p (i k m) -> p i k m", i=2, k=KD)
        x_first = wa[:, KD * 3 * D:KD * 4 * D].rearrange("p (k c) -> p k c", k=KD)
        xT = hx[:, 0:KD * N].rearrange("p (n k c) -> p n k c", n=NC_, k=KD)
        x_parts = hx[:, 0:KD * N].bitcast(F16).rearrange("p (n i k c) -> p n i k c", n=NC_, i=2, k=KD)
        hs = hx[:, :].rearrange("p (k l c) -> p k l c", l=L + 1, k=KD)
        hs_s = hx[:, :].rearrange("p (k l b s) -> p k l b s", k=KD, l=L + 1, s=SEG)
        HID_RING = 4
        tokrow = hx[:, 0:NG * ROW].rearrange("p (g d) -> p g d", g=NG)
        y = hx[:, NG * ROW:NG * (ROW + D)].rearrange("p (g d) -> p g d", g=NG)
        hid_full = hx[:, NG * (ROW + D):NG * (ROW + D) + HID_RING * CAP].rearrange("p (m c) -> p m c", m=HID_RING)
        gone = [0]

        def gru_tmp(n):
            gone[0] += n
            return wb[:, gone[0] - n:gone[0]]
        pre = gru_tmp(2 * KD * COLS).rearrange("p (j g c) -> p j g c", j=KD, g=2)
        rz = gru_tmp(2 * KD * COLS).rearrange("p (j g c) -> p j g c", j=KD, g=2)
        rn = gru_tmp(KD * COLS).rearrange("p (j c) -> p j c", j=KD)
        cand_in = gru_tmp(KD * COLS).rearrange("p (j c) -> p j c", j=KD)
        cand = gru_tmp(KD * COLS).rearrange("p (j c) -> p j c", j=KD)
        zh = gru_tmp(KD * COLS).rearrange("p (j c) -> p j c", j=KD)
        ocand = gru_tmp(KD * COLS).rearrange("p (j c) -> p j c", j=KD)
        halves = gru_tmp(2 * KD * COLS).bitcast(F16).rearrange("p (i k h c) -> p i k h c", i=2, k=KD, h=2)
        gap = wb[:, 0:KD * COLS]
        gap_s = gap.rearrange("p (k b s) -> p k b s", k=KD, s=SEG)
        assert gone[0] <= KD * 3 * D

        assert later[0] <= 3 * KD * N

        ident = sb("ident", [P, P])
        ones = sb("ones", [P, P])
        onesb = sb("onesb", [P, P], BF16)
        before = sb("before", [P, P], BF16)
        same = sb("same", [P, P], BF16)
        first_step = sb("first_step", [P, P], BF16)
        bih = sb("bih", [P, 12])
        bhh = sb("bhh", [P, 12])
        bsum = sb("bsum", [P, 12])
        h0 = sb("h0", [P, KD, NB])
        wg_sb = sb("wg_sb", [P, KD, E])
        bg_sb = sb("bg_sb", [P, E])
        peak = sb("peak", [P, 6])
        peak_all = sb("peak_all", [P, 6])
        scale = sb("scale", [P, 6])
        unscale = sb("unscale", [P, 6])
        un_gi = sb("un_gi", [P, 1])
        chunk_peak = sb("chunk_peak", [P, 4])
        hid_scale = sb("hid_scale", [P, 1])
        un_hid_in = sb("un_hid_in", [P, 1])
        un_y = sb("un_y", [P, 1])
        gates_scale = sb("gates_scale", [P, 1])
        un_gates = sb("un_gates", [P, 1])
        bhn_s = sb("bhn_s", [P, KD])
        neg_scale = sb("neg_scale", [P, 1])
        worst = sb("worst", [P, 4])
        flag = sb("flag", [P, SEG + 1], I32)
        lg = sb("lg", [P, NT, E])
        earlier = sb("earlier", [P, E, E])
        rank = sb("rank", [P, NT, E])
        lmax = sb("lmax", [P, NT])
        wsum = sb("wsum", [P, NT])
        prob = sb("prob", [P, NT, E])
        score = sb("score", [P, E, NT])
        steps_i = sb("steps_i", [P, SEARCH_PASSES, NCAND], I32)
        trial = sb("trial", [P, E, NCAND], I32)
        keep = sb("keep", [P, E, NCAND])
        thr = sb("thr", [P, E])
        gt = sb("gt", [P, E, NT], BF16)
        eqp = sb("eqp", [P, E, 2 * NT], BF16)
        selp = sb("selp", [P, E, 2 * NT], BF16)
        fits = sb("fits", [P, E, NT], BF16)
        pos = sb("pos", [P, E, NT])
        slot_no = sb("slot_no", [P, CAP], F16)
        tok_id = sb("tok_id", [P, NT], F16)
        idx = sb("idx", [P, NG], I32)
        idx_out = sb("idx_out", [P, NG], I32)
        p_out = sb("p_out", [P, NG])

        turn = sb("turn", [P, KD, P + E])
        turn_ps = ps[:, :, 0:2 * (P + E)].rearrange("p (n b) (k c) -> p n b k c", b=2, k=2)
        gate_ps = ps[:, 0:4, 0:3 * COLS].rearrange("p j (g c) -> p j g c", g=3)

        names = """
            small_loaded whh_loaded x_loaded out_init consts_pool consts_dve bias_ready gi_mm gi_ready gi_scaled
            wih_high wih_split x_high x_split peak_ready peak_known chain whh_ready zh_done high_ready
            state_done low_ready last_low_ready gates_mm pre_ready sig_done rn_done candin_ready tanh_done
            ocand_done start_saved check_a worst_ready worst_mm flag_ready gru_over turned probs_in rows_copied
            rows_stored steps_made exp_in exp_done above_ready turn_ready shares_added chunk_peaks total_mm
            masks_ready eq_mm sel_ready pos_mm slots_ready list_mm idx_ready gathered tok_turned tokT_ready
            ffn1_mm hid_ready ffn2_mm y_ready scattered latched w_peak w_peak_all w_scaled w_high w_low prep
            hid_made hid_high tok_high tables sp_waited pool_waited dve_waited pe_waited act_waited pool_consts""".split()
        S = {name: sem(name) for name in names}
        S["stage_loaded"] = [sem(f"stage_loaded_{c}") for c in range(4)]
        S["wih_loaded"] = [sem(f"wih_loaded_{g}") for g in range(3)]
        block = ctx.enter_context(nc.Block())

        whh_src = w_hh.rearrange("(k p) m -> p k m", p=P)
        wih_src = w_ih.rearrange("(k p) m -> p k m", p=P)
        w_src = {W1: w1.rearrange("e (c p) h -> e p c h", p=P),
                 W2: w2.rearrange("e (c k p) d -> e p c k d", p=P, c=CHUNKS)}
        rows_dst = hs_rows.rearrange("(c n v) d -> v c n d", v=2, c=COLS)
        ROWS_B = 4

        HIGH, LOW = 0, 1
        W2_SPLIT_AT = (4, 6, 8, 10)

        PRODUCTS = ((HIGH, HIGH), (HIGH, LOW), (LOW, HIGH))

        EXACT = {HIGH: (HIGH, LOW), LOW: (HIGH,)}
        GUESS = {HIGH: (HIGH,), LOW: ()}

        ORDER = ((HIGH, 0, 0), (HIGH, 1, 0), (HIGH, 2, 0), (HIGH, 0, 1), (HIGH, 1, 1), (HIGH, 2, 1),
                 (HIGH, 3, 0), (HIGH, 3, 1), (LOW, 0, 0), (LOW, 1, 0), (LOW, 2, 0), (LOW, 3, 0),
                 (HIGH, 0, 2), (HIGH, 1, 2), (HIGH, 2, 2), (HIGH, 0, 3), (LOW, 0, 1), (LOW, 0, 2),
                 (LOW, 0, 3), (HIGH, 1, 3), (LOW, 1, 1), (LOW, 1, 2), (LOW, 1, 3), (HIGH, 2, 3),
                 (LOW, 2, 1), (LOW, 2, 2), (LOW, 2, 3), (HIGH, 3, 2), (HIGH, 3, 3), (LOW, 3, 1),
                 (LOW, 3, 2), (LOW, 3, 3))

        MADE_ROUND, STEPS_ROUND = KD * (L + 1), KD * L
        MADE_1, STEPS_1 = KD * (BURN + 1), KD * BURN
        MADE_2, STEPS_2 = MADE_1 + MADE_ROUND, STEPS_1 + STEPS_ROUND
        MADE_3, STEPS_3 = MADE_2 + MADE_ROUND, STEPS_2 + STEPS_ROUND

        @block.sync
        def _(sp):
            sp.dma_start(x_first, x_t[:, 0, :, :]).then_inc(S["x_loaded"], 16)
            for g in range(3):
                sp.dma_start(wih_sb[:, :, g * D:(g + 1) * D], wih_src[:, :, g * D:(g + 1) * D]
                             ).then_inc(S["wih_loaded"][g], 16)
            for n in range(1, NC_):
                sp.wait_ge(S["x_loaded"], 16 * n)
                sp.dma_start(xT[:, n, :, :], x_t[:, n, :, :]).then_inc(S["x_loaded"], 16)
            sp.wait_ge(S["gi_mm"], 12)
            sp.wait_ge(S["wih_split"], KD)
            for k in range(KD):
                sp.dma_start(whh_sb[:, k, :], whh_src[:, k, :]).then_inc(S["whh_loaded"], 16)
            sp.dma_start(out.rearrange("b t d -> (b t) d"), x.rearrange("b t d -> (b t) d")).then_inc(S["out_init"], 16)
            sp.wait_ge(S["gru_over"], 1)

            def load(which, e, fetched):
                for c in range(CHUNKS):
                    if not (isinstance(fetched, int) and fetched == 0):
                        sp.wait_ge(S["w_low"], 2 * CHUNKS * fetched + (2 * c + 2 - 2 * CHUNKS))
                        sp.sem_inc(S["sp_waited"], 1)
                    dst = stage[:, c * CHUNK:(c + 1) * CHUNK]
                    src = w_src[which][bass.ds(e, 1), :, c]
                    if which == W1:
                        src = src.rearrange("o p h -> (o p) h")
                    else:
                        src = src.rearrange("o p k d -> (o p) k d")
                        dst = dst.rearrange("p (k d) -> p k d", d=D)
                    sp.dma_start(dst, src).then_inc(S["stage_loaded"][c], 16)

            load(W1, 0, 0)
            sp.wait_ge(S["probs_in"], 1)
            for n in range(0, NT, ROWS_B):
                sp.wait_ge(S["rows_copied"], n + ROWS_B)
                for v in range(2):
                    sp.dma_start(rows_dst[v, :, n:n + ROWS_B], rows[v * COLS:(v + 1) * COLS, n:n + ROWS_B, :]
                                 ).then_inc(S["rows_stored"], 16)
            load(W2, 0, 1)
            with sp.Fori(1, E) as e:
                load(W1, e, 2 * e)
                load(W2, e, 2 * e + 1)
            sp.wait_ge(S["out_init"], 16)
            sp.wait_ge(S["rows_stored"], 32 * (NT // ROWS_B))
            sp.wait_ge(S["scattered"], 16 * NG * E)

        @block.tensor
        def _(pe):
            pe.wait_ge(S["consts_pool"], 1)
            pe.wait_ge(S["x_loaded"], 16)
            for m in range(12):
                if m >= 4:
                    pe.wait_ge(S["gi_ready"], m - 3)
                if m % 4 == 0:
                    pe.wait_ge(S["wih_loaded"][m // 4], 16)
                for k in range(KD):
                    mm = pe.matmul(ps[:, m % 4, :], wih_sb[:, k, m * P:(m + 1) * P], x_first[:, k, :],
                                   start=(k == 0), stop=(k == KD - 1))
                mm.then_inc(S["gi_mm"], 1)
            pe.wait_ge(S["wih_split"], KD)
            with pe.Fori(0, NC_ - 1) as i:
                pe.wait_ge(S["x_split"], i + 1)
                for m in range(12):
                    pe.wait_ge(S["gi_ready"], i * 12 + (12 + m - 3))
                    for k in range(KD):
                        for n, (w, t) in enumerate(PRODUCTS):
                            mm = pe.matmul(ps[:, m % 4, :], wih_parts[:, w, k, m * P:(m + 1) * P],
                                           x_parts[:, bass.ds(i, 1), t, k, :].rearrange("p o c -> p (o c)"),
                                           start=(k == 0 and n == 0), stop=(k == KD - 1 and n == 2))
                    mm.then_inc(S["gi_mm"], 1)

            def gates(src, base, steps, products):
                seen = set()
                last_part = LOW if products[LOW] else HIGH
                for h, j, k in ORDER:
                    if not products[h]:
                        continue
                    if k == 0 and h == HIGH and j >= 2:
                        pe.wait_ge(S["rn_done"], steps + j + 1)
                    first = (h, k) not in seen
                    seen.add((h, k))
                    if first and h == HIGH:
                        pe.wait_ge(S["high_ready"], base + k + 1)
                    if first and h == LOW and k < KD - 1:
                        pe.wait_ge(S["low_ready"], base + k + 1)
                    if first and h == LOW and k == KD - 1:
                        pe.wait_ge(S["last_low_ready"], base + KD)
                    for w in products[h]:
                        for g in range(3):
                            mm = pe.matmul(gate_ps[:, j, g, :], whh_parts[:, k, w, (4 * g + j) * P:(4 * g + j + 1) * P],
                                           halves[:, src, k, h, :], start=(k == 0 and g == 0 and h == HIGH and w == HIGH),
                                           stop=(k == KD - 1 and h == last_part and w == products[h][-1]),
                                           skip_group_check=True)
                    if k == KD - 1 and h == last_part:
                        mm.then_inc(S["gates_mm"], 1)

            pe.wait_ge(S["whh_ready"], KD)
            pe.wait_ge(S["gi_ready"], 12 * NC_)

            def run(base, steps, n, products):
                with pe.Fori(0, n // 2) as i:
                    for u in range(2):
                        gates(u, base + 8 * i + 4 * u, steps + 8 * i + 4 * u, products)

            run(0, 0, BURN, GUESS)
            run(MADE_1, STEPS_1, ROUGH, GUESS)
            run(MADE_1 + KD * ROUGH, STEPS_1 + KD * ROUGH, L - ROUGH, EXACT)

            def any_apart(count):
                pe.wait_ge(S["worst_ready"], count)
                pe.matmul(ps[0:1, 4, 0:1], worst[:, 2:3], ones[:, 0:1], start=True, stop=True).then_inc(S["worst_mm"], 1)

            run(MADE_2, STEPS_2, L, EXACT)
            any_apart(1)
            pe.wait_ge(S["flag_ready"], 1)
            pe.sem_inc(S["pe_waited"], 1)
            more = pe.value_load(flag[0:1, 0:1])
            with pe.If(more > 0):
                with pe.Fori(0, SEG - 1) as r:
                    pe.wait_ge(S["flag_ready"], r + 1)
                    pe.sem_inc(S["pe_waited"], 1)
                    go = pe.value_load(flag[0:1, bass.ds(r, 1)])
                    with pe.If(go > 0):
                        run(r * MADE_ROUND + MADE_3, r * STEPS_ROUND + STEPS_3, L, EXACT)
                        any_apart(r + 2)

            def states_of(n, k):
                return hs[:, k, 2 * n + 1:2 * n + 3, :].rearrange("p l c -> p (l c)")

            pe.wait_ge(S["gru_over"], 1)
            pe.wait_ge(S["turn_ready"], 1)
            for n in range(NT):
                if n >= 4:
                    pe.wait_ge(S["rows_copied"], n - 3)
                    pe.wait_ge(S["shares_added"], n - 3)
                for k in range(KD):
                    mm = pe.matmul(turn_ps[:, n % 4, k // 2, k % 2, :], states_of(n, k), turn[:, k, :], start=True, stop=True)
                mm.then_inc(S["turned"], 1)
            with pe.Fori(0, SEARCH_PASSES) as i:
                pe.wait_ge(S["above_ready"], i + 1)
                for n in range(NT):
                    mm = pe.matmul(ps[:, 6, 0:E * NCAND], onesb[:, :], above[:, n, :, :].rearrange("p e c -> p (e c)"),
                                   start=(n == 0), stop=(n == NT - 1))
                mm.then_inc(S["total_mm"], 1)

            def earlier_count(bank, maskp, more):
                o = ps[:, bank, 0:E * NT].rearrange("p (e n) -> p e n", e=E)
                for n in range(NT):
                    pe.matmul(o, before[:, :], maskp[:, :, NT + n:NT + n + 1].to_broadcast([P, E, NT]),
                              start=(n == 0), stop=False)
                for d in range(1, NT):
                    pe.matmul(o, same[:, :], maskp[:, :, NT - d:2 * NT - d], start=False, stop=False)
                mm = pe.matmul(o, first_step[:, :], maskp[:, :, NT:2 * NT], start=False, stop=not more)
                if more:
                    for n in range(NT):
                        mm = pe.matmul(o, onesb[:, :], gt[:, :, n:n + 1].to_broadcast([P, E, NT]), start=False,
                                       stop=(n == NT - 1))
                return mm

            pe.wait_ge(S["masks_ready"], 1)
            earlier_count(7, eqp, True).then_inc(S["eq_mm"], 1)
            pe.wait_ge(S["sel_ready"], 1)
            earlier_count(7, selp, False).then_inc(S["pos_mm"], 1)

            def token_list(e):
                for n in range(NT):
                    pe.wait_ge(S["slots_ready"], NT * e + n + 1)
                    for g in range(NG):
                        mm = pe.matmul(ps[:, 6, g:g + 1], slots[:, n, g * P:(g + 1) * P], tok_id[:, n:n + 1],
                                       start=(n == 0 and g == 0), stop=(n == NT - 1), skip_group_check=True)
                mm.then_inc(S["list_mm"], 1)

            def turn_tokens(e):
                pe.wait_ge(S["gathered"], 16 * NG * e + 16 * NG)
                for g in range(NG):
                    for k in range(KD):
                        mm = pe.transpose(ps[:, 4 + g, k * P:(k + 1) * P], tokrow[:, g, k * P:(k + 1) * P],
                                          ident[:, :])
                    mm.then_inc(S["tok_turned"], 1)

            def expert(e, last):
                pe.wait_ge(S["tokT_ready"], NG * e + NG)
                pe.wait_ge(S["w_low"], 4 * CHUNKS * e + 2 * CHUNKS)
                for m in range(KH):
                    if m >= 2:
                        pe.wait_ge(S["hid_made"], KH * e + m - 1)
                    for k in range(KD):
                        for n, (w, t) in enumerate(PRODUCTS):
                            mm = pe.matmul(ps[:, m % 2, :], w1p[:, w, k, m * P:(m + 1) * P], tokT[:, t, k, :],
                                           start=(k == 0 and n == 0), stop=(k == KD - 1 and n == 2))
                    mm.then_inc(S["ffn1_mm"], 1)
                    if m == 10 and not last:
                        token_list(e + 1)
                pe.wait_ge(S["w_low"], 4 * CHUNKS * e + 4 * CHUNKS)
                for g in range(NG):
                    if g >= 2:
                        pe.wait_ge(S["y_ready"], NG * e + g - 1)
                    for k in range(KH):
                        if g == 0:
                            pe.wait_ge(S["hid_ready"], KH * e + k + 1)
                        for n, (w, h) in enumerate(PRODUCTS):
                            mm = pe.matmul(ps[:, 2 + g % 2, :], hid[:, h, k, g * P:(g + 1) * P], w2p[:, w, k, :],
                                           start=(k == 0 and n == 0), stop=(k == KH - 1 and n == 2))
                    mm.then_inc(S["ffn2_mm"], 1)
                    if g == 1 and not last:
                        turn_tokens(e + 1)

            token_list(0)
            turn_tokens(0)
            with pe.Fori(0, E - 1) as e:
                expert(e, False)
            expert(E - 1, True)

        @block.scalar
        def _(act):
            act.dma_start(bih[:, :], b_ih).then_inc(S["small_loaded"], 16)
            act.dma_start(bhh[:, :], b_hh).then_inc(S["small_loaded"], 16)
            act.dma_start(h0[:, :, :], cond_t).then_inc(S["small_loaded"], 16)
            act.dma_start(wg_sb[:, :, :], wg).then_inc(S["small_loaded"], 16)
            act.dma_start(bg_sb[:, :], bg.rearrange("(o e) -> o e", o=1).to_broadcast([P, E])).then_inc(S["small_loaded"], 16)
            act.wait_ge(S["consts_dve"], 1)
            act.activation(worst[:, 3:4], ones[:, 0:1], ACT.Sigmoid).then_inc(S["tables"], 1)
            act.wait_ge(S["tables"], 1)

            act.wait_ge(S["bias_ready"], 1)

            def wih_high(k):
                act.activation(wih_parts[:, HIGH, k, :], wih_sb[:, k, :], ACT.Copy,
                               scale=scale[:, WIH:WIH + 1]).then_inc(S["wih_high"], 1)

            def x_high(n):
                if n >= 2:
                    act.wait_ge(S["x_split"], n - 1)
                act.activation(x_parts[:, n - 1, HIGH, :, :], xT[:, n, :, :], ACT.Copy,
                               scale=scale[:, X:X + 1]).then_inc(S["x_high"], 1)

            for m in range(12):
                act.wait_ge(S["gi_mm"], m + 1)
                act.activation(gi[:, m % 4, m // 4, 0:GCOLS], ps[:, m % 4, :], ACT.Identity,
                               bias=bsum[:, m:m + 1]).then_inc(S["gi_ready"], 1)
                if m == 6:
                    act.wait_ge(S["gi_scaled"], 1)
                if 6 <= m < 6 + KD:
                    wih_high(m - 6)
                if m == 10:
                    x_high(1)
            for n in range(2, NC_):
                x_high(n)
            with act.Fori(0, NC_ - 1) as i:
                for m in range(12):
                    act.wait_ge(S["gi_mm"], i * 12 + (12 + m + 1))
                    act.activation(gi[:, m % 4, m // 4, bass.ds(i * GCOLS + GCOLS, GCOLS)], ps[:, m % 4, :], ACT.Identity,
                                   bias=bsum[:, m:m + 1], scale=un_gi[:, 0:1]).then_inc(S["gi_ready"], 1)

            def step(l, base):
                def sig(j):
                    act.wait_ge(S["pre_ready"], base + j + 1)
                    act.activation(rz[:, j, :, :], pre[:, j, :, :], ACT.Sigmoid,
                                   scale=un_gates[:, 0:1]).then_inc(S["sig_done"], 1)

                def tanh(j):
                    act.wait_ge(S["candin_ready"], base + j + 1)
                    act.activation(cand[:, j, :], cand_in[:, j, :], ACT.Tanh,
                                   scale=un_gates[:, 0:1]).then_inc(S["tanh_done"], 1)
                for f, j in ((sig, 0), (sig, 1), (tanh, 0), (sig, 2), (tanh, 1), (sig, 3), (tanh, 2), (tanh, 3)):
                    f(j)

            def run(l0, steps, n):
                with act.Fori(0, n // 2) as i:
                    for u in range(2):
                        step(2 * i + (l0 + u), steps + 8 * i + 4 * u)

            run(L - BURN, 0, BURN)
            run(0, STEPS_1, L)
            run(0, STEPS_2, L)
            act.wait_ge(S["flag_ready"], 1)
            act.sem_inc(S["act_waited"], 1)
            more = act.value_load(flag[0:1, 0:1])
            with act.If(more > 0):
                with act.Fori(0, SEG - 1) as r:
                    act.wait_ge(S["flag_ready"], r + 1)
                    act.sem_inc(S["act_waited"], 1)
                    go = act.value_load(flag[0:1, bass.ds(r, 1)])
                    with act.If(go > 0):
                        run(0, r * STEPS_ROUND + STEPS_3, L)

            for n in range(NT):
                act.wait_ge(S["turned"], n + 1)
                act.wait_ge(S["shares_added"], n + 1)
                act.copy(rows[:, n, 0:D].rearrange("p (b k c) -> p b k c", b=2, k=2), turn_ps[:, n % 4, :, :, 0:P]
                         ).then_inc(S["rows_copied"], 1)
            act.wait_ge(S["exp_in"], 1)
            act.activation(prob[:, :, :], lg[:, :, :], ACT.Exp).then_inc(S["exp_done"], 1)

            def w_high(which, c, order):
                if c == 0:
                    act.wait_ge(S["w_scaled"], order + 1)
                act.activation(w_parts[which][:, HIGH, c * CHUNK:(c + 1) * CHUNK], stage[:, c * CHUNK:(c + 1) * CHUNK],
                               ACT.Copy, scale=scale[:, which:which + 1]).then_inc(S["w_high"], 1)

            def tokens_high(e):
                for g in range(NG):
                    act.wait_ge(S["tok_turned"], NG * e + g + 1)
                    act.copy(tokT[:, HIGH, :, g * P:(g + 1) * P],
                             ps[:, 4 + g, :].rearrange("p (k c) -> p k c", k=KD)).then_inc(S["tok_high"], 1)

            def hidden(e):
                for m in range(KH):
                    act.wait_ge(S["ffn1_mm"], KH * e + m + 1)
                    if m >= HID_RING:
                        act.wait_ge(S["hid_ready"], KH * e + m - HID_RING + 1)
                    act.activation(hid_full[:, m % HID_RING, :], ps[:, m % 2, :], ACT.Gelu,
                                   scale=un_hid_in[:, 0:1]).then_inc(S["hid_made"], 1)
                    act.wait_ge(S["hid_made"], KH * e + m + 1)
                    act.activation(hid[:, HIGH, m, :], hid_full[:, m % HID_RING, :], ACT.Copy,
                                   scale=hid_scale[:, 0:1]).then_inc(S["hid_high"], 1)
                    if m in W2_SPLIT_AT:
                        w_high(W2, W2_SPLIT_AT.index(m), 2 * e + 1)

            for c in range(CHUNKS):
                w_high(W1, c, 0)
            tokens_high(0)
            with act.Fori(0, E - 1) as e:
                hidden(e)
                for c in range(CHUNKS):
                    w_high(W1, c, 2 * e + 2)
                tokens_high(e + 1)
            hidden(E - 1)

        @block.gpsimd
        def _(pool):
            pool.memset(ident[:, :], 0.0).then_inc(S["pool_consts"], 1)
            pool.wait_ge(S["pool_consts"], 1)
            pool.affine_select(out=ident[:, :], in_=ident[:, :], compare_op=ALU.not_equal, fill=1.0, base=0,
                               pattern=[[-1, P]], channel_multiplier=1).then_inc(S["consts_pool"], 1)
            pool.memset(before[:, :], 0.0).then_inc(S["pool_consts"], 1)
            pool.wait_ge(S["pool_consts"], 2)
            columns = before[:, :].rearrange("p (v c) -> p v c", v=2)
            pool.affine_select(out=columns, in_=columns, compare_op=ALU.is_ge, fill=1.0, base=-COLS,
                               pattern=[[0, 2], [-1, COLS]], channel_multiplier=1).then_inc(S["pool_consts"], 1)
            pool.wait_ge(S["pool_consts"], 3)
            pool.memset(before[0:COLS, :], 0.0).then_inc(S["pool_consts"], 1)
            pool.wait_ge(S["pool_consts"], 4)
            pool.affine_select(out=columns[0:COLS], in_=columns[0:COLS], compare_op=ALU.is_ge, fill=1.0, base=0,
                               pattern=[[0, 2], [-1, COLS]], channel_multiplier=1).then_inc(S["consts_pool"], 1)
            pool.wait_ge(S["consts_pool"], 2)
            pool.iota(slot_no[:, :], [[1, CAP]], base=0, channel_multiplier=0,
                      allow_small_or_imprecise_dtypes=True).then_inc(S["consts_pool"], 1)
            pool.wait_ge(S["consts_pool"], 3)
            pool.iota(tok_id[:, :], [[2, NT]], base=1 - COLS * L, channel_multiplier=L,
                      allow_small_or_imprecise_dtypes=True).then_inc(S["pool_consts"], 1)
            pool.wait_ge(S["pool_consts"], 5)
            pool.iota(tok_id[0:COLS, :], [[2, NT]], base=0, channel_multiplier=L,
                      allow_small_or_imprecise_dtypes=True).then_inc(S["consts_pool"], 1)
            pool.wait_ge(S["consts_pool"], 4)
            pool.memset(earlier[:, :, :], 0.0).then_inc(S["pool_consts"], 1)
            pool.wait_ge(S["pool_consts"], 6)
            pool.affine_select(out=earlier[:, :, :], in_=earlier[:, :, :], compare_op=ALU.is_ge, fill=1.0, base=0,
                               pattern=[[-1, E], [1, E]], channel_multiplier=0).then_inc(S["consts_pool"], 1)
            pool.wait_ge(S["peak_ready"], 1)
            pool.partition_all_reduce(peak_all[:, WIH:X + 1], peak[:, WIH:X + 1], P, RMAX).then_inc(S["peak_known"], 1)
            pool.wait_ge(S["peak_ready"], 2)
            pool.partition_all_reduce(peak_all[:, 0:2], peak[:, 0:2], P, RMAX).then_inc(S["peak_known"], 1)

            def step(l, dst, base):
                def carry(j):
                    pool.wait_ge(S["sig_done"], base + j + 1)
                    pool.sem_inc(S["pool_waited"], 1)
                    pool.tensor_tensor(zh[:, j, :], rz[:, j, 1, :], hs[:, j, bass.ds(l, 1), :].rearrange("p o c -> p (o c)"),
                                       ALU.mult).then_inc(S["zh_done"], 1)

                def low(j):
                    pool.wait_ge(S["state_done"], base + j + 1)
                    pool.sem_inc(S["pool_waited"], 1)
                    pool.tensor_tensor(halves[:, dst, j, LOW, :], hs[:, j, bass.ds(l + 1, 1), :].rearrange("p o c -> p (o c)"),
                                       halves[:, dst, j, HIGH, :], ALU.subtract
                                       ).then_inc(S["low_ready"], 2 if j == KD - 2 else 1)
                for f, j in ((carry, 0), (carry, 1), (carry, 2), (carry, 3), (low, 0), (low, 1), (low, 2)):
                    f(j)

            def run(l0, steps, n):
                with pool.Fori(0, n // 2) as i:
                    for u in range(2):
                        step(2 * i + (l0 + u), 1 - u, steps + 8 * i + 4 * u)

            run(L - BURN, 0, BURN)
            run(0, STEPS_1, L)
            run(0, STEPS_2, L)
            pool.wait_ge(S["flag_ready"], 1)
            pool.sem_inc(S["pool_waited"], 1)
            more = pool.value_load(flag[0:1, 0:1])
            with pool.If(more > 0):
                with pool.Fori(0, SEG - 1) as r:
                    pool.wait_ge(S["flag_ready"], r + 1)
                    pool.sem_inc(S["pool_waited"], 1)
                    go = pool.value_load(flag[0:1, bass.ds(r, 1)])
                    with pool.If(go > 0):
                        run(0, r * STEPS_ROUND + STEPS_3, L)

            def gather(e):
                pool.wait_ge(S["idx_ready"], e + 1)
                pool.sem_inc(S["pool_waited"], 1)
                for g in range(NG):
                    pool.indirect_dma_start(
                        out=tokrow[:, g, :], out_offset=None, in_=hs_rows,
                        in_offset=bass.IndirectOffsetOnAxis(ap=idx[:, g:g + 1], axis=0)).then_inc(S["gathered"], 16)

            def scatter(e, g):
                pool.wait_ge(S["y_ready"], NG * e + g + 1)
                pool.sem_inc(S["pool_waited"], 1)
                pool.indirect_dma_start(
                    out=out.rearrange("b t d -> (b t) d"),
                    out_offset=bass.IndirectOffsetOnAxis(ap=idx_out[:, g:g + 1], axis=0),
                    in_=y[:, g, :], in_offset=None, compute_op=ALU.add).then_inc(S["scattered"], 16)

            def peak_of(which, order):
                pool.wait_ge(S["w_peak"], order + 1)
                pool.sem_inc(S["pool_waited"], 1)
                pool.partition_all_reduce(peak_all[:, which:which + 1], peak[:, which:which + 1], P, RMAX
                                          ).then_inc(S["w_peak_all"], 1)

            peak_of(W1, 0)
            pool.wait_ge(S["rows_stored"], 32 * (NT // ROWS_B))
            pool.wait_ge(S["out_init"], 16)
            gather(0)
            peak_of(W2, 1)
            with pool.Fori(0, E - 1) as e:
                pool.wait_ge(S["latched"], e + 1)
                pool.sem_inc(S["pool_waited"], 1)
                gather(e + 1)
                peak_of(W1, 2 * e + 2)
                scatter(e, 0)
                scatter(e, 1)
                scatter(e, 2)
                peak_of(W2, 2 * e + 3)
                scatter(e, 3)
            for g in range(NG):
                scatter(E - 1, g)

        @block.vector
        def _(dve):
            dve.memset(ones[:, :], 1.0).then_inc(S["consts_dve"], 1)
            dve.memset(onesb[:, :], 1.0)
            dve.memset(flag[:, :], 0)
            dve.memset(eqp[:, :, 0:NT], 0.0)
            dve.memset(selp[:, :, 0:NT], 0.0)
            dve.sem_inc(S["rn_done"], KD)
            for i in range(SEARCH_PASSES):
                shift = SEARCH_BITS * (SEARCH_PASSES - 1 - i)
                for c in range(NCAND):
                    ins = dve.memset(steps_i[:, i, c:c + 1], c << shift)
            ins.then_inc(S["steps_made"], 1)
            dve.wait_ge(S["steps_made"], 1)
            dve.wait_ge(S["small_loaded"], 16 * 5)
            dve.wait_ge(S["consts_pool"], 1)
            for k in range(KD):
                dve.tensor_copy(turn[:, k, 0:P], ident[:, :])
            dve.tensor_copy(turn[:, :, P:P + E], wg_sb[:, :, :]).then_inc(S["turn_ready"], 1)
            dve.tensor_tensor(bsum[:, 0:8], bih[:, 0:8], bhh[:, 0:8], ALU.add)
            dve.tensor_copy(bsum[:, 8:12], bih[:, 8:12]).then_inc(S["bias_ready"], 1)
            dve.wait_ge(S["bias_ready"], 1)

            link_n = [0]

            def link(ins):
                link_n[0] += 1
                ins.then_inc(S["chain"], 1)
                dve.wait_ge(S["chain"], link_n[0])

            def pow2(cols):
                link(dve.tensor_scalar(peak_all[:, cols], peak_all[:, cols], 1e-30, None, ALU.max))
                link(dve.tensor_scalar(unscale[:, cols].bitcast(I32), peak_all[:, cols].bitcast(I32), 0x7F800000, None,
                                       ALU.bitwise_and))
                dve.tensor_scalar(scale[:, cols].bitcast(I32), unscale[:, cols].bitcast(I32), -1.0,
                                  float((254 + SCALE_TO) << 23), ALU.mult, ALU.add)
                link(dve.tensor_scalar(unscale[:, cols].bitcast(I32), unscale[:, cols].bitcast(I32),
                                       -float(SCALE_TO << 23), None, ALU.add))

            for g in range(3):
                dve.wait_ge(S["wih_loaded"][g], 16)
            dve.tensor_reduce(peak[:, WIH:WIH + 1], wih_sb, AX.XY, ALU.max, apply_absolute_value=True)
            dve.wait_ge(S["x_loaded"], 16 * NC_)
            link(dve.tensor_reduce(peak[:, X:X + 1], hx[:, KD * GCOLS:KD * N], AX.X, ALU.max, apply_absolute_value=True))
            dve.sem_inc(S["peak_ready"], 1)
            dve.wait_ge(S["peak_known"], 1)
            pow2(slice(WIH, X + 1))
            link(dve.tensor_tensor(un_gi[:, :], unscale[:, WIH:WIH + 1], unscale[:, X:X + 1], ALU.mult))
            dve.sem_inc(S["gi_scaled"], 1)
            for k in range(KD):
                dve.wait_ge(S["wih_high"], k + 1)
                dve.scalar_tensor_tensor(wih_parts[:, LOW, k, :], wih_sb[:, k, :], scale[:, WIH:WIH + 1],
                                         wih_parts[:, HIGH, k, :], ALU.mult, ALU.subtract).then_inc(S["wih_split"], 1)
            for n in range(1, NC_):
                dve.wait_ge(S["x_high"], n)
                dve.scalar_tensor_tensor(x_parts[:, n - 1, LOW, :, :], xT[:, n, :, :], scale[:, X:X + 1],
                                         x_parts[:, n - 1, HIGH, :, :], ALU.mult, ALU.subtract).then_inc(S["x_split"], 1)

            dve.tensor_reduce(peak[:, STATE:STATE + 1], h0[:, :, :], AX.XY, ALU.max, apply_absolute_value=True)
            dve.wait_ge(S["whh_loaded"], 16 * KD)
            link(dve.tensor_reduce(peak[:, WHH:WHH + 1], whh_sb, AX.XY, ALU.max, apply_absolute_value=True))
            link(dve.tensor_scalar(peak[:, STATE:STATE + 1], peak[:, STATE:STATE + 1], 1.0, None, ALU.max))
            dve.sem_inc(S["peak_ready"], 1)
            dve.wait_ge(S["peak_known"], 2)
            pow2(slice(WHH, STATE + 1))
            dve.tensor_tensor(un_gates[:, :], unscale[:, WHH:WHH + 1], unscale[:, STATE:STATE + 1], ALU.mult)
            link(dve.tensor_tensor(gates_scale[:, :], scale[:, WHH:WHH + 1], scale[:, STATE:STATE + 1], ALU.mult))
            dve.tensor_scalar(neg_scale[:, :], scale[:, STATE:STATE + 1], -1.0, None, ALU.mult)
            link(dve.tensor_scalar(bhn_s[:, :], bhh[:, 8:12], gates_scale[:, 0:1], None, ALU.mult))
            for k in range(KD):
                link(dve.tensor_scalar(parts_tmp[:, HIGH, :], whh_sb[:, k, :], scale[:, WHH:WHH + 1], None, ALU.mult))
                link(dve.scalar_tensor_tensor(parts_tmp[:, LOW, :], whh_sb[:, k, :], scale[:, WHH:WHH + 1],
                                              parts_tmp[:, HIGH, :], ALU.mult, ALU.subtract))
                link(dve.tensor_copy(whh_parts[:, k, :, :], parts_tmp[:, :, :]))
                dve.sem_inc(S["whh_ready"], 1)
            with dve.Fori(0, NC_) as c:
                for m in range(12):
                    dve.wait_ge(S["gi_ready"], c * 12 + m + 1)
                    dve.tensor_scalar(gi[:, m % 4, m // 4, bass.ds(c * GCOLS, GCOLS)],
                                      gi[:, m % 4, m // 4, bass.ds(c * GCOLS, GCOLS)],
                                      gates_scale[:, 0:1], None, ALU.mult)
            dve.wait_ge(S["gi_mm"], 12 * NC_)
            dve.memset(hs[:, :, L - BURN, :], 0.0)
            link(dve.memset(halves[:, 0, :, :, :], 0.0))
            dve.sem_inc(S["high_ready"], KD)
            dve.sem_inc(S["low_ready"], KD)
            dve.sem_inc(S["last_low_ready"], KD)

            def step(l, src, base):
                col = l * COLS
                dst = 1 - src

                def pre_rz(j):
                    dve.wait_ge(S["gates_mm"], base + j + 1)
                    dve.tensor_tensor(pre[:, j, :, :], gate_ps[:, j, 0:2, :], gi[:, j, 0:2, bass.ds(col, COLS)],
                                      ALU.add).then_inc(S["pre_ready"], 1)

                def reset(j):
                    dve.wait_ge(S["sig_done"], base + j + 1)
                    dve.scalar_tensor_tensor(rn[:, j, :], gate_ps[:, j, 2, :], bhn_s[:, j:j + 1], rz[:, j, 0, :],
                                             ALU.add, ALU.mult).then_inc(S["rn_done"], 1)

                def candidate_in(j):
                    dve.wait_ge(S["rn_done"], base + (KD + j + 1))
                    dve.tensor_tensor(cand_in[:, j, :], rn[:, j, :], gi[:, j, 2, bass.ds(col, COLS)],
                                      ALU.add).then_inc(S["candin_ready"], 1)

                def one_less_z(j):
                    dve.wait_ge(S["tanh_done"], base + j + 1)
                    dve.scalar_tensor_tensor(ocand[:, j, :], rz[:, j, 1, :], -1.0, cand[:, j, :],
                                             ALU.add, ALU.mult).then_inc(S["ocand_done"], 1)

                def blend(j):
                    dve.wait_ge(S["zh_done"], base + j + 1)
                    dve.wait_ge(S["ocand_done"], base + j + 1)
                    dve.scalar_tensor_tensor(halves[:, dst, j, HIGH, :], ocand[:, j, :], neg_scale[:, 0:1], zh[:, j, :],
                                             ALU.mult, ALU.add).then_inc(S["high_ready"], 1)

                def keep_state(j):
                    dve.scalar_tensor_tensor(hs[:, j, bass.ds(l + 1, 1), :].rearrange("p o c -> p (o c)"), ocand[:, j, :],
                                             neg_scale[:, 0:1], zh[:, j, :], ALU.mult, ALU.add).then_inc(S["state_done"], 1)

                def last_low(j):
                    dve.wait_ge(S["state_done"], base + j + 1)
                    dve.tensor_tensor(halves[:, dst, j, LOW, :], hs[:, j, bass.ds(l + 1, 1), :].rearrange("p o c -> p (o c)"),
                                      halves[:, dst, j, HIGH, :], ALU.subtract).then_inc(S["last_low_ready"], KD)
                for f, j in ((pre_rz, 0), (pre_rz, 1), (reset, 0), (pre_rz, 2), (candidate_in, 0),
                             (reset, 1), (pre_rz, 3), (candidate_in, 1), (one_less_z, 0), (reset, 2),
                             (blend, 0), (one_less_z, 1), (candidate_in, 2), (reset, 3), (blend, 1),
                             (keep_state, 0), (candidate_in, 3), (one_less_z, 2), (keep_state, 1), (blend, 2),
                             (one_less_z, 3), (keep_state, 2), (blend, 3), (keep_state, 3), (last_low, 3)):
                    f(j)

            def next_start(count):
                for k in range(KD):
                    ins = dve.tensor_copy(hs_s[:, k, 0, :, 1:SEG], hs_s[:, k, L, :, 0:SEG - 1])
                ins.then_inc(S["start_saved"], 1)
                dve.wait_ge(S["start_saved"], 3 * count + 1)
                dve.tensor_copy(halves[:, 0, :, HIGH, :], hs[:, :, 0, :]).then_inc(S["start_saved"], 1)
                dve.wait_ge(S["start_saved"], 3 * count + 2)
                dve.sem_inc(S["high_ready"], KD)
                dve.tensor_tensor(halves[:, 0, :, LOW, :], hs[:, :, 0, :], halves[:, 0, :, HIGH, :],
                                  ALU.subtract).then_inc(S["start_saved"], 1)
                dve.wait_ge(S["start_saved"], 3 * count + 3)
                dve.sem_inc(S["low_ready"], KD)
                dve.sem_inc(S["last_low_ready"], KD)

            def run(l0, steps, n):
                with dve.Fori(0, n // 2) as i:
                    for u in range(2):
                        step(2 * i + (l0 + u), u, steps + 8 * i + 4 * u)

            run(L - BURN, 0, BURN)
            link(dve.tensor_scalar(hs_s[:, :, 0, :, 0:1], h0[:, :, :].unsqueeze(3), scale[:, STATE:STATE + 1], None, ALU.mult))
            dve.wait_ge(S["low_ready"], MADE_1)
            dve.wait_ge(S["state_done"], STEPS_1)
            next_start(0)
            run(0, STEPS_1, L)
            dve.wait_ge(S["low_ready"], MADE_2)
            dve.wait_ge(S["state_done"], STEPS_2)
            next_start(1)

            def check(count):
                dve.wait_ge(S["low_ready"], count * MADE_ROUND + (MADE_2 + MADE_ROUND))
                dve.wait_ge(S["state_done"], count * STEPS_ROUND + (STEPS_2 + STEPS_ROUND))
                for k in range(KD):
                    dve.tensor_tensor(gap_s[:, k, :, 0:SEG - 1], hs_s[:, k, L, :, 0:SEG - 1], hs_s[:, k, 0, :, 1:SEG],
                                      ALU.subtract)
                dve.tensor_reduce(worst[:, 1:2], hs[:, :, L, :], AX.XY, ALU.max, apply_absolute_value=True
                                  ).then_inc(S["check_a"], 2)
                dve.wait_ge(S["check_a"], 4 * count + 2)
                dve.tensor_reduce(worst[:, 0:1], gap_s[:, :, :, 0:SEG - 1], AX.XYZ, ALU.max, apply_absolute_value=True
                                  ).then_inc(S["check_a"], 1)
                dve.wait_ge(S["check_a"], 4 * count + 3)
                dve.scalar_tensor_tensor(worst[:, 2:3], worst[:, 1:2], TOL, worst[:, 0:1],
                                         ALU.mult, ALU.is_lt).then_inc(S["worst_ready"], 1)
                next_start(count + 2)
                dve.wait_ge(S["worst_mm"], count + 1)
                dve.tensor_copy(flag[0:1, bass.ds(count, 1)], ps[0:1, 4, 0:1]).then_inc(S["check_a"], 1)
                dve.wait_ge(S["check_a"], 4 * count + 4)
                dve.sem_inc(S["dve_waited"], 1)

            run(0, STEPS_2, L)
            check(0)
            dve.sem_inc(S["flag_ready"], 1)
            more = dve.value_load(flag[0:1, 0:1])
            with dve.If(more > 0):
                with dve.Fori(0, SEG - 1) as r:
                    go = dve.value_load(flag[0:1, bass.ds(r, 1)])
                    with dve.If(go > 0):
                        run(0, r * STEPS_ROUND + STEPS_3, L)
                        check(r + 1)
                    dve.sem_inc(S["flag_ready"], 1)
            dve.sem_inc(S["gru_over"], 1)

            PREPS = 4

            def find_peak(which, order):
                for c in range(CHUNKS):
                    chunk_max(which, c, order)
                whole_max(which, order)

            def chunk_max(which, c, order):
                dve.wait_ge(S["stage_loaded"][c], 16 * order + 16)
                dve.tensor_reduce(chunk_peak[:, c:c + 1], stage[:, c * CHUNK:(c + 1) * CHUNK], AX.X, ALU.max,
                                  apply_absolute_value=True).then_inc(S["chunk_peaks"], 1)

            def whole_max(which, order):
                dve.wait_ge(S["chunk_peaks"], CHUNKS * order + CHUNKS)
                dve.tensor_reduce(peak[:, which:which + 1], chunk_peak[:, :], AX.X, ALU.max).then_inc(S["w_peak"], 1)

            def set_scale(which, order):
                col = slice(which, which + 1)
                dve.wait_ge(S["w_peak_all"], order + 1)
                dve.tensor_scalar(peak_all[:, col], peak_all[:, col], 1e-30, None, ALU.max).then_inc(S["prep"], 1)
                dve.wait_ge(S["prep"], PREPS * order + 1)
                dve.tensor_scalar(unscale[:, col].bitcast(I32), peak_all[:, col].bitcast(I32), 0x7F800000, None,
                                  ALU.bitwise_and).then_inc(S["prep"], 1)
                dve.wait_ge(S["prep"], PREPS * order + 2)
                dve.tensor_scalar(scale[:, col].bitcast(I32), unscale[:, col].bitcast(I32), -1.0,
                                  float((254 + SCALE_TO) << 23), ALU.mult, ALU.add)
                dve.tensor_scalar(unscale[:, col].bitcast(I32), unscale[:, col].bitcast(I32),
                                  -float(SCALE_TO << 23), None, ALU.add).then_inc(S["prep"], 1)
                dve.wait_ge(S["prep"], PREPS * order + 3)

            def w1_scales(order):
                dve.tensor_tensor(un_hid_in[:, :], unscale[:, W1:W1 + 1], unscale[:, STATE:STATE + 1], ALU.mult)
                dve.scalar_tensor_tensor(hid_scale[:, :], scale[:, W1:W1 + 1], HIDDEN_TO, scale[:, STATE:STATE + 1],
                                         ALU.mult, ALU.mult).then_inc(S["prep"], 1)
                dve.wait_ge(S["prep"], PREPS * order + 4)
                dve.sem_inc(S["w_scaled"], 1)

            def w2_scales(order):
                dve.scalar_tensor_tensor(un_y[:, :], un_hid_in[:, :], 1.0 / HIDDEN_TO, unscale[:, W2:W2 + 1],
                                         ALU.mult, ALU.mult).then_inc(S["prep"], 1)
                dve.wait_ge(S["prep"], PREPS * order + 4)
                dve.sem_inc(S["w_scaled"], 1)

            def w_low(which, c, order):
                dve.wait_ge(S["w_high"], CHUNKS * order + c + 1)
                cols = slice(c * CHUNK, (c + 1) * CHUNK)
                dve.scalar_tensor_tensor(w_parts[which][:, LOW, cols], stage[:, cols], scale[:, which:which + 1],
                                         w_parts[which][:, HIGH, cols], ALU.mult, ALU.subtract).then_inc(S["w_low"], 2)

            dve.wait_ge(S["consts_pool"], 5)
            for v in range(2):
                dve.tensor_copy(same[v * COLS:(v + 1) * COLS, 0:COLS], ident[v * COLS:(v + 1) * COLS, v * COLS:(v + 1) * COLS])
                dve.tensor_copy(same[v * COLS:(v + 1) * COLS, COLS:P], ident[v * COLS:(v + 1) * COLS, v * COLS:(v + 1) * COLS])
            link(dve.memset(first_step[:, :], 0.0))
            dve.tensor_copy(first_step[0:COLS, COLS:P], ident[0:COLS, 0:COLS])
            mine = lg[:, :, :].unsqueeze(3).to_broadcast([P, NT, E, E])
            other = lg[:, :, :].unsqueeze(2).to_broadcast([P, NT, E, E])
            for n in range(NT):
                dve.wait_ge(S["turned"], n + 1)
                dve.tensor_reduce(lg[:, n, :], turn_ps[:, n % 4, :, :, P:P + E].rearrange("p b k e -> p e b k"), AX.XY,
                                  ALU.add).then_inc(S["shares_added"], 1)
                if n % 4 == 3 and n < NT - 1:
                    chunk_max(W1, n // 4, 0)
            dve.wait_ge(S["shares_added"], NT)
            link(dve.scalar_tensor_tensor(lg[:, :, :], lg[:, :, :], unscale[:, STATE:STATE + 1],
                                          bg_sb[:, :].unsqueeze(1).to_broadcast([P, NT, E]), ALU.mult, ALU.add))
            dve.tensor_tensor(cmp4[:, :, :, :], other, mine, ALU.is_gt)
            dve.tensor_tensor(cmp5[:, :, :, :], other, mine, ALU.is_equal)
            link(dve.tensor_reduce(lmax[:, :], lg[:, :, :], AX.X, ALU.max))
            link(dve.tensor_tensor(cmp5[:, :, :, :], cmp5[:, :, :, :],
                                   earlier[:, :, :].unsqueeze(1).to_broadcast([P, NT, E, E]), ALU.mult))
            dve.tensor_tensor(lg[:, :, :], lg[:, :, :], lmax[:, :].unsqueeze(2).to_broadcast([P, NT, E]),
                              ALU.subtract).then_inc(S["exp_in"], 1)
            link(dve.tensor_tensor(cmp4[:, :, :, :], cmp4[:, :, :, :], cmp5[:, :, :, :], ALU.add))
            link(dve.tensor_reduce(rank[:, :, :], cmp4[:, :, :, :], AX.X, ALU.add))
            chunk_max(W1, 3, 0)
            whole_max(W1, 0)
            dve.wait_ge(S["exp_done"], 1)
            set_scale(W1, 0)
            w1_scales(0)
            link(dve.scalar_tensor_tensor(prob[:, :, :], rank[:, :, :], 2.0, prob[:, :, :], ALU.is_lt, ALU.mult))
            link(dve.tensor_reduce(wsum[:, :], prob[:, :, :], AX.X, ALU.add))
            link(dve.reciprocal(wsum[:, :], wsum[:, :]))
            link(dve.tensor_tensor(prob[:, :, :], prob[:, :, :], wsum[:, :].unsqueeze(2).to_broadcast([P, NT, E]),
                                   ALU.mult))
            dve.tensor_copy(score[:, :, :], prob[:, :, :].rearrange("p n e -> p e n"))
            link(dve.memset(thr[:, :], 0.0))
            dve.tensor_copy(rows[:, :, D:ROW], prob[:, :, :]).then_inc(S["probs_in"], 1)

            base = link_n[0]

            def search(i, chunk):
                dve.tensor_tensor(trial[:, :, :], thr[:, :].bitcast(I32).unsqueeze(2).to_broadcast([P, E, NCAND]),
                                  steps_i[:, bass.ds(i, 1), :].to_broadcast([P, E, NCAND]),
                                  ALU.bitwise_or).then_inc(S["chain"], 1)
                dve.wait_ge(S["chain"], 3 * i + (base + 1))
                dve.tensor_tensor(above[:, :, :, :], prob[:, :, :].unsqueeze(3).to_broadcast([P, NT, E, NCAND]),
                                  trial[:, :, :].bitcast(F32).unsqueeze(1).to_broadcast([P, NT, E, NCAND]),
                                  ALU.is_ge).then_inc(S["above_ready"], 1)
                if chunk is not None:
                    dve.wait_ge(S["w_high"], chunk + 1)
                    cols = bass.ds(i * (CHUNK // 2), CHUNK // 2)
                    dve.scalar_tensor_tensor(w_parts[W1][:, LOW, cols], stage[:, cols], scale[:, W1:W1 + 1],
                                             w_parts[W1][:, HIGH, cols], ALU.mult, ALU.subtract).then_inc(S["w_low"], 1)
                dve.wait_ge(S["total_mm"], i + 1)
                dve.scalar_tensor_tensor(keep[:, :, :], ps[:, 6, 0:E * NCAND].rearrange("p (e c) -> p e c", e=E),
                                         float(CAP), trial[:, :, :].bitcast(F32), ALU.is_ge,
                                         ALU.mult).then_inc(S["chain"], 1)
                dve.wait_ge(S["chain"], 3 * i + (base + 2))
                dve.tensor_reduce(thr[:, :], keep[:, :, :], AX.X, ALU.max).then_inc(S["chain"], 1)
                dve.wait_ge(S["chain"], 3 * i + (base + 3))

            with dve.Fori(0, CHUNKS) as c:
                for u in range(2):
                    search(2 * c + u, c)
            for i in range(2 * CHUNKS, SEARCH_PASSES):
                search(i, None)
            link_n[0] += 3 * SEARCH_PASSES

            thr_b = thr[:, :].unsqueeze(2).to_broadcast([P, E, NT])
            ps7 = ps[:, 7, 0:E * NT].rearrange("p (e n) -> p e n", e=E)
            dve.tensor_tensor(gt[:, :, :], score[:, :, :], thr_b, ALU.is_gt)
            link(dve.tensor_tensor(eqp[:, :, NT:2 * NT], score[:, :, :], thr_b, ALU.is_equal))
            dve.sem_inc(S["masks_ready"], 1)
            dve.wait_ge(S["eq_mm"], 1)
            link(dve.scalar_tensor_tensor(fits[:, :, :], ps7, float(CAP), eqp[:, :, NT:2 * NT], ALU.is_lt, ALU.mult))
            link(dve.tensor_tensor(selp[:, :, NT:2 * NT], fits[:, :, :], gt[:, :, :], ALU.add))
            dve.sem_inc(S["sel_ready"], 1)
            dve.wait_ge(S["pos_mm"], 1)
            link(dve.scalar_tensor_tensor(pos[:, :, :], ps7, 1.0, selp[:, :, NT:2 * NT], ALU.add, ALU.mult))
            link(dve.tensor_scalar(pos[:, :, :], pos[:, :, :], -1.0, None, ALU.add))

            def one_hot(e, blocks):
                for n in blocks:
                    dve.tensor_scalar(slots[:, n, :], slot_no[:, :], pos[:, bass.ds(e, 1), n:n + 1].rearrange("p o n -> p (o n)"),
                                      None, ALU.is_equal).then_inc(S["slots_ready"], 1)

            def make_idx(e):
                dve.wait_ge(S["list_mm"], e + 1)
                dve.tensor_copy(idx[:, :], ps[:, 6, 0:NG]).then_inc(S["idx_ready"], 1)

            def tokens_low(e):
                for g in range(NG):
                    dve.wait_ge(S["tok_high"], NG * e + g + 1)
                    dve.tensor_tensor(tokT[:, LOW, :, g * P:(g + 1) * P],
                                      ps[:, 4 + g, :].rearrange("p (k c) -> p k c", k=KD),
                                      tokT[:, HIGH, :, g * P:(g + 1) * P], ALU.subtract).then_inc(S["tokT_ready"], 1)

            def latch(e):
                dve.tensor_copy(idx_out[:, :], idx[:, :])
                dve.tensor_copy(p_out[:, :], tokrow[:, :, bass.ds(D + e, 1)].rearrange("p g o -> p (g o)")
                                ).then_inc(S["latched"], 1)
                dve.wait_ge(S["latched"], e + 1)

            def hidden_low(e, m):
                dve.wait_ge(S["hid_high"], KH * e + m + 1)
                dve.scalar_tensor_tensor(hid[:, LOW, m, :], hid_full[:, m % HID_RING, :], hid_scale[:, 0:1],
                                         hid[:, HIGH, m, :], ALU.mult, ALU.subtract).then_inc(S["hid_ready"], 1)

            def weigh(e, g):
                dve.wait_ge(S["ffn2_mm"], NG * e + g + 1)
                dve.tensor_scalar(y[:, g, :], ps[:, 2 + g % 2, :], un_y[:, 0:1], p_out[:, g:g + 1],
                                  ALU.mult, ALU.mult).then_inc(S["y_ready"], 1)

            def first_product(e, last):
                for m in range(KH):
                    hidden_low(e, m)
                    if m < 4 and not last:
                        one_hot(e + 1, range(4 * m, 4 * m + 4))
                    if m in W2_SPLIT_AT:
                        w_low(W2, W2_SPLIT_AT.index(m), 2 * e + 1)
                    if m == 12 and not last:
                        make_idx(e + 1)

            one_hot(0, range(NT))
            make_idx(0)
            find_peak(W2, 1)
            tokens_low(0)
            latch(0)
            set_scale(W2, 1)
            w2_scales(1)
            with dve.Fori(0, E - 1) as e:
                first_product(e, False)
                find_peak(W1, 2 * e + 2)
                weigh(e, 0)
                set_scale(W1, 2 * e + 2)
                w1_scales(2 * e + 2)
                w_low(W1, 0, 2 * e + 2)
                w_low(W1, 1, 2 * e + 2)
                weigh(e, 1)
                w_low(W1, 2, 2 * e + 2)
                w_low(W1, 3, 2 * e + 2)
                tokens_low(e + 1)
                weigh(e, 2)
                find_peak(W2, 2 * e + 3)
                weigh(e, 3)
                set_scale(W2, 2 * e + 3)
                w2_scales(2 * e + 3)
                dve.wait_ge(S["scattered"], 16 * NG * e + 16 * NG)
                latch(e + 1)
            first_product(E - 1, True)
            for g in range(NG):
                weigh(E - 1, g)


def laid_out(inputs):
    x = np.asarray(inputs['x'])
    nb, t, d = x.shape
    kd, steps = d // P, t // SEG
    x_t = x.reshape(nb * SEG, steps, kd, P).transpose(3, 2, 1, 0).reshape(P, kd, -1, 512).transpose(0, 2, 1, 3)
    return {
        'x': x,
        'x_t': x_t,
        'cond_t': np.asarray(inputs['cond_2048']).reshape(nb, kd, P).transpose(2, 1, 0),
        'w_ih': inputs['L0_cond_W_ih'],
        'w_hh': inputs['L0_cond_W_hh'],
        'b_ih': np.asarray(inputs['L0_cond_b_ih']).reshape(-1, P).T,
        'b_hh': np.asarray(inputs['L0_cond_b_hh']).reshape(-1, P).T,
        'wg': np.asarray(inputs['L0_ffn_Wg']).reshape(kd, P, -1).transpose(1, 0, 2),
        'bg': inputs['L0_ffn_bg'],
        'w1': inputs['L0_ffn_W1'],
        'w2': inputs['L0_ffn_W2'],
    }


def kernel(**inputs):
    import concourse.bacc as bacc
    from concourse.bass_utils import run_bass_kernel_spmd

    nc = bacc.Bacc("TRN2", target_bir_lowering=False, num_devices=1)
    arrays, args = {}, []
    for name, a in laid_out(inputs).items():
        a = np.ascontiguousarray(a)
        arrays[f"in_{name}"] = a
        args.append(nc.dram_tensor(f"in_{name}", a.shape, mybir.dt.from_np(a.dtype), kind="ExternalInput").ap())
    shape = inputs['x'].shape
    experts = inputs['L0_ffn_Wg'].shape[1]
    hs_rows = nc.dram_tensor("hs_rows", (shape[0] * shape[1], shape[2] + experts), F32, kind="Internal").ap()
    out = nc.dram_tensor("out_0", shape, F32, kind="ExternalOutput").ap()
    gru_moe(nc, *args, hs_rows, out)
    r = run_bass_kernel_spmd(nc, [arrays], core_ids=[0])
    return r.results[0]["out_0"]
```
